# Optimizing a Trainium2 kernel written in Bass

```python
import numpy as np
import jax
import jax.numpy as jnp

def _softmax(x, axis=-1):
    return jax.nn.softmax(x, axis=axis)

def _gelu(x):
    return jax.nn.gelu(x, approximate=True)

def _silu(x):
    return jax.nn.silu(x)

def _sigmoid(x):
    return jax.nn.sigmoid(x)

def _layernorm(x, axis=-1, eps=1e-05):
    m = jnp.mean(x, axis=axis, keepdims=True)
    v = jnp.var(x, axis=axis, keepdims=True)
    return (x - m) / jnp.sqrt(v + eps)

def _scatter_add(tgt, idx, src, axis=0):
    return tgt.at[idx].add(src)

def _segment_sum(src, seg, n):
    return jax.ops.segment_sum(src, seg, n)
kernel_name = 'mk_seq_postln_d1_jaxref_r4_0d8c9d'

def setup_inputs(seed: int=0):
    np.random.seed(seed)
    _w = jnp.asarray

    def _L0_attn_setup():
        import jax, jax.numpy as jnp
        import numpy as np
        D_MODEL = 512
        D_STATE = 128
        D_CONV = 4
        EXPAND = 2
        D_HEAD = 64
        D_INNER = EXPAND * D_MODEL
        N_HEADS = D_INNER // D_HEAD
        CONV_DIM = D_INNER + 2 * D_STATE
        D_IN_PROJ = 2 * D_INNER + 2 * D_STATE + N_HEADS
        CHUNK = 64
        EPS = 1e-05

        def _forward(u, W_in, conv_w, conv_b, dt_bias, A_log, Dp, norm_w, W_out):
            b, l, _ = u.shape
            zxbcdt = u @ W_in.T
            z = zxbcdt[..., :D_INNER]
            xBC = zxbcdt[..., D_INNER:D_INNER + CONV_DIM]
            dt = zxbcdt[..., D_INNER + CONV_DIM:]
            xpad = jnp.pad(xBC, ((0, 0), (D_CONV - 1, 0), (0, 0)))
            xBC = sum((xpad[:, w:w + l, :] * conv_w[:, w] for w in range(D_CONV))) + conv_b
            xBC = jax.nn.silu(xBC)
            x = xBC[..., :D_INNER]
            Bm = xBC[..., D_INNER:D_INNER + D_STATE]
            Cm = xBC[..., D_INNER + D_STATE:]
            dt = jax.nn.softplus(dt + dt_bias)
            A = -jnp.exp(A_log)
            c = l // CHUNK
            dtc = dt.reshape(b, c, CHUNK, (h_ := N_HEADS))
            dA_cs = jnp.cumsum(dtc * A, axis=2)
            xc = x.reshape(b, c, CHUNK, N_HEADS, D_HEAD)
            Bc = Bm.reshape(b, c, CHUNK, D_STATE)
            Cc = Cm.reshape(b, c, CHUNK, D_STATE)
            mask = jnp.tril(jnp.ones((CHUNK, CHUNK), bool))
            diff = dA_cs[:, :, :, None, :] - dA_cs[:, :, None, :, :]
            L = jnp.exp(jnp.where(mask[None, None, :, :, None], diff, -jnp.inf))
            CB = jnp.einsum('bcin,bcjn->bcij', Cc, Bc)
            M = CB[..., None] * L * dtc[:, :, None, :, :]
            y_diag = jnp.einsum('bcijh,bcjhp->bcihp', M, xc)
            decay_last = jnp.exp(dA_cs[:, :, -1:, :] - dA_cs)
            states = jnp.einsum('bcsh,bcsn,bcshp->bchpn', decay_last * dtc, Bc, xc)
            chunk_decay = jnp.exp(dA_cs[:, :, -1, :])

            def step(s, inp):
                st, dec = inp
                return (s * dec[:, :, None, None] + st, s)
            s0 = jnp.zeros((b, N_HEADS, D_HEAD, D_STATE), u.dtype)
            _, prev = jax.lax.scan(step, s0, (states.transpose(1, 0, 2, 3, 4), chunk_decay.transpose(1, 0, 2)))
            prev = prev.transpose(1, 0, 2, 3, 4)
            y_off = jnp.einsum('bcin,bchpn,bcih->bcihp', Cc, prev, jnp.exp(dA_cs))
            y = y_diag + y_off + Dp[None, None, None, :, None] * xc
            y = y.reshape(b, l, D_INNER)
            yg = y * jax.nn.silu(z)
            yg = yg * jax.lax.rsqrt(jnp.mean(yg * yg, axis=-1, keepdims=True) + EPS)
            y = yg * norm_w
            return y @ W_out.T
        key = jax.random.key(seed)
        ks = jax.random.split(key, 8)
        B, L = (2, 1024)
        u = jax.random.normal(ks[0], (B, L, D_MODEL), jnp.float32)
        W_in = 0.02 * jax.random.normal(ks[1], (D_IN_PROJ, D_MODEL), jnp.float32)
        conv_w = 0.1 * jax.random.normal(ks[2], (CONV_DIM, D_CONV), jnp.float32)
        conv_b = jnp.zeros((CONV_DIM,), jnp.float32)
        dt = jnp.exp(jax.random.uniform(ks[3], (N_HEADS,)) * (np.log(0.1) - np.log(0.001)) + np.log(0.001))
        dt = jnp.clip(dt, 0.0001, None)
        dt_bias = dt + jnp.log(-jnp.expm1(-dt))
        A_log = jnp.log(jax.random.uniform(ks[4], (N_HEADS,), minval=1.0, maxval=16.0))
        Dp = jnp.ones((N_HEADS,), jnp.float32)
        norm_w = jnp.ones((D_INNER,), jnp.float32)
        W_out = 0.02 * jax.random.normal(ks[5], (D_MODEL, D_INNER), jnp.float32)
        return {'u': u, 'W_in': W_in, 'conv_w': conv_w, 'conv_b': conv_b, 'dt_bias': dt_bias, 'A_log': A_log, 'Dp': Dp, 'norm_w': norm_w, 'W_out': W_out}
    _L0_attn_in = _L0_attn_setup()

    def _L0_ffn_setup():
        import jax, jax.numpy as jnp
        import numpy as np
        D_MODEL = 512
        D_EXPERT = 2048
        EPS = 1e-08

        def ternary_quant(w):
            scale = jnp.mean(jnp.abs(w)) + EPS
            q = jnp.clip(jnp.round(w / scale), -1.0, 1.0) * scale
            return w + jax.lax.stop_gradient(q - w)
        key = jax.random.key(seed)
        k_x, k_up, k_gate, k_down = jax.random.split(key, 4)
        std_in = 1.0 / np.sqrt(D_MODEL)
        std_exp = 1.0 / np.sqrt(D_EXPERT)
        return {'x': jax.random.normal(k_x, (4, 512, D_MODEL), dtype=jnp.float32), 'W_up': jax.random.normal(k_up, (D_EXPERT, D_MODEL), dtype=jnp.float32) * std_in, 'W_gate': jax.random.normal(k_gate, (D_EXPERT, D_MODEL), dtype=jnp.float32) * std_in, 'W_down': jax.random.normal(k_down, (D_MODEL, D_EXPERT), dtype=jnp.float32) * std_exp}
    _L0_ffn_in = _L0_ffn_setup()
    _d = {'L0_attn_u': _L0_attn_in['u'], 'L0_attn_W_in': _L0_attn_in['W_in'], 'L0_attn_conv_w': _L0_attn_in['conv_w'], 'L0_attn_conv_b': _L0_attn_in['conv_b'], 'L0_attn_dt_bias': _L0_attn_in['dt_bias'], 'L0_attn_A_log': _L0_attn_in['A_log'], 'L0_attn_Dp': _L0_attn_in['Dp'], 'L0_attn_norm_w': _L0_attn_in['norm_w'], 'L0_attn_W_out': _L0_attn_in['W_out'], 'L0_ffn_W_up': _L0_ffn_in['W_up'], 'L0_ffn_W_gate': _L0_ffn_in['W_gate'], 'L0_ffn_W_down': _L0_ffn_in['W_down']}
    _x0 = _d['L0_attn_u']
    _d['L0_attn_u'] = jax.random.normal(jax.random.fold_in(jax.random.key(seed), 1), (4, 1024, 512), dtype=_x0.dtype)
    del _x0
    return _d

def reference(L0_attn_u, L0_attn_W_in, L0_attn_conv_w, L0_attn_conv_b, L0_attn_dt_bias, L0_attn_A_log, L0_attn_Dp, L0_attn_norm_w, L0_attn_W_out, L0_ffn_W_up, L0_ffn_W_gate, L0_ffn_W_down):

    def _L0_attn_ref(u, W_in, conv_w, conv_b, dt_bias, A_log, Dp, norm_w, W_out):
        import jax, jax.numpy as jnp
        import numpy as np
        D_MODEL = 512
        D_STATE = 128
        D_CONV = 4
        EXPAND = 2
        D_HEAD = 64
        D_INNER = EXPAND * D_MODEL
        N_HEADS = D_INNER // D_HEAD
        CONV_DIM = D_INNER + 2 * D_STATE
        D_IN_PROJ = 2 * D_INNER + 2 * D_STATE + N_HEADS
        CHUNK = 64
        EPS = 1e-05

        def _forward(u, W_in, conv_w, conv_b, dt_bias, A_log, Dp, norm_w, W_out):
            b, l, _ = u.shape
            zxbcdt = u @ W_in.T
            z = zxbcdt[..., :D_INNER]
            xBC = zxbcdt[..., D_INNER:D_INNER + CONV_DIM]
            dt = zxbcdt[..., D_INNER + CONV_DIM:]
            xpad = jnp.pad(xBC, ((0, 0), (D_CONV - 1, 0), (0, 0)))
            xBC = sum((xpad[:, w:w + l, :] * conv_w[:, w] for w in range(D_CONV))) + conv_b
            xBC = jax.nn.silu(xBC)
            x = xBC[..., :D_INNER]
            Bm = xBC[..., D_INNER:D_INNER + D_STATE]
            Cm = xBC[..., D_INNER + D_STATE:]
            dt = jax.nn.softplus(dt + dt_bias)
            A = -jnp.exp(A_log)
            c = l // CHUNK
            dtc = dt.reshape(b, c, CHUNK, (h_ := N_HEADS))
            dA_cs = jnp.cumsum(dtc * A, axis=2)
            xc = x.reshape(b, c, CHUNK, N_HEADS, D_HEAD)
            Bc = Bm.reshape(b, c, CHUNK, D_STATE)
            Cc = Cm.reshape(b, c, CHUNK, D_STATE)
            mask = jnp.tril(jnp.ones((CHUNK, CHUNK), bool))
            diff = dA_cs[:, :, :, None, :] - dA_cs[:, :, None, :, :]
            L = jnp.exp(jnp.where(mask[None, None, :, :, None], diff, -jnp.inf))
            CB = jnp.einsum('bcin,bcjn->bcij', Cc, Bc)
            M = CB[..., None] * L * dtc[:, :, None, :, :]
            y_diag = jnp.einsum('bcijh,bcjhp->bcihp', M, xc)
            decay_last = jnp.exp(dA_cs[:, :, -1:, :] - dA_cs)
            states = jnp.einsum('bcsh,bcsn,bcshp->bchpn', decay_last * dtc, Bc, xc)
            chunk_decay = jnp.exp(dA_cs[:, :, -1, :])

            def step(s, inp):
                st, dec = inp
                return (s * dec[:, :, None, None] + st, s)
            s0 = jnp.zeros((b, N_HEADS, D_HEAD, D_STATE), u.dtype)
            _, prev = jax.lax.scan(step, s0, (states.transpose(1, 0, 2, 3, 4), chunk_decay.transpose(1, 0, 2)))
            prev = prev.transpose(1, 0, 2, 3, 4)
            y_off = jnp.einsum('bcin,bchpn,bcih->bcihp', Cc, prev, jnp.exp(dA_cs))
            y = y_diag + y_off + Dp[None, None, None, :, None] * xc
            y = y.reshape(b, l, D_INNER)
            yg = y * jax.nn.silu(z)
            yg = yg * jax.lax.rsqrt(jnp.mean(yg * yg, axis=-1, keepdims=True) + EPS)
            y = yg * norm_w
            return y @ W_out.T
        return _forward(u, W_in, conv_w, conv_b, dt_bias, A_log, Dp, norm_w, W_out)

    def _L0_ffn_ref(x, W_up, W_gate, W_down):
        import jax, jax.numpy as jnp
        import numpy as np
        D_MODEL = 512
        D_EXPERT = 2048
        EPS = 1e-08

        def ternary_quant(w):
            scale = jnp.mean(jnp.abs(w)) + EPS
            q = jnp.clip(jnp.round(w / scale), -1.0, 1.0) * scale
            return w + jax.lax.stop_gradient(q - w)
        wu = ternary_quant(W_up)
        wg = ternary_quant(W_gate)
        wd = ternary_quant(W_down)
        up = jnp.einsum('bsd,ed->bse', x, wu)
        gate = jnp.einsum('bsd,ed->bse', x, wg)
        hidden = jax.nn.silu(up) * gate
        return jnp.einsum('bse,de->bsd', hidden, wd)
    x = L0_attn_u
    x = _layernorm(x + _L0_attn_ref(x, L0_attn_W_in, L0_attn_conv_w, L0_attn_conv_b, L0_attn_dt_bias, L0_attn_A_log, L0_attn_Dp, L0_attn_norm_w, L0_attn_W_out), axis=-1)
    x = _layernorm(x + _L0_ffn_ref(x, L0_ffn_W_up, L0_ffn_W_gate, L0_ffn_W_down), axis=-1)
    return x

_drawn_inputs = setup_inputs


def setup_inputs(seed=0):
    import zlib

    import numpy as np

    out = dict(_drawn_inputs(seed))
    spreads = {'L0_attn_conv_b': (0.0, 0.1), 'L0_attn_Dp': (1.0, 0.2), 'L0_attn_norm_w': (1.0, 0.2)}
    factors = {}
    for name, (base, spread) in spreads.items():
        noise = np.random.default_rng([zlib.crc32(name.encode()), seed]).standard_normal(out[name].shape)
        drawn = base * np.exp(spread * noise) if base else spread * noise
        out[name] = jnp.asarray(drawn.astype(out[name].dtype))
    for name, factor in factors.items():
        out[name] = (out[name] * factor).astype(out[name].dtype)
    return out
```

```python
from contextlib import ExitStack
from itertools import cycle

import concourse.bass as bass
from concourse import mybir

ALU = mybir.AluOpType
ACT = mybir.ActivationFunctionType
AX = mybir.AxisListType
F32 = mybir.dt.float32
F16 = mybir.dt.float16
F8 = mybir.dt.float8e4
RED = bass.bass_isa.ReduceOp

P = 128
U_TOP = 1024.0
W_TOP = 256.0
A_GAIN = 256.0
A_FLOOR = -60000.0
NORM_GAIN = 1024.0
HID_GAIN = 1.0 / 8.0
LN_EPS = 1e-5
RMS_EPS = 1e-5
QUANT_EPS = 1e-8
TINY = 1e-30


class Line:

    def __init__(self, clock, eng, sem, step=1):
        self.clock, self.eng, self.sem, self.step = clock, eng, sem, step
        self.count = 0
        self.seen = {}
        clock.lines.append(self)

    def did(self, ins):
        ins.then_inc(self.sem, self.step)
        self.count += self.step
        return (self.clock.epoch, self, self.count)

    def wait(self, *marks):
        for m in marks:
            if m is None:
                continue
            if isinstance(m, list):
                self.wait(*m)
                continue
            epoch, line, value = m
            if epoch == self.clock.epoch and self.seen.get(line.sem, 0) < value:
                self.eng.wait_ge(line.sem, value)
                self.seen[line.sem] = value

    def now(self):
        return (self.clock.epoch, self, self.count) if self.count else None


class Clock:
    def __init__(self):
        self.epoch = 0
        self.lines = []

    def turn(self):
        self.epoch += 1
        for line in self.lines:
            line.count = 0
            line.seen = {}


def drain(*steps):
    total = max(n for _, n in steps)
    done = [0] * len(steps)
    for k in range(1, total + 1):
        for i, (gen, n) in enumerate(steps):
            while done[i] < (k * n + total - 1) // total:
                next(gen, None)
                done[i] += 1
    for gen, _ in steps:
        for _ in gen:
            pass


def build(nc, u, uT, W_inT, conv_w, conv_b, dt_bias, A_log, Dp, norm_w, W_outT, W_upT, W_gateT, W_downT, out):
    B, L, D = u.shape
    DI = W_outT.shape[0]
    H = Dp.shape[0]
    CD = conv_w.shape[0]
    NS = (CD - DI) // 2
    HD = DI // H
    DE = W_upT.shape[1]
    DP = W_inT.shape[1]
    TAPS = conv_w.shape[1]
    HALO = TAPS - 1
    T = 512
    NT = B * L // T
    NC = T // P
    KD = D // P
    CT = CD // P
    XT = DI // P
    ET = DE // P
    EH = ET // 2
    ZW = DI // T
    HB = T // HD
    HQ = T // P
    assert L == 2 * T and NS == P and DI % T == 0 and D == T and HD * 2 == P

    clock = Clock()
    with ExitStack() as ctx:
        def sb(name, shape, dt=F32):
            return ctx.enter_context(nc.sbuf_tensor(name, shape, dt))

        ident = sb("ident", [P, P])
        tri_le = sb("tri_le", [P, P])
        tri_gt = sb("tri_gt", [P, P])
        ones = sb("ones", [P, P])
        tri_le16 = sb("tri_le16", [P, P], F16)
        tri_gt16 = sb("tri_gt16", [P, P], F16)
        minus_half = sb("minus_half", [P, 1])
        cw = sb("cw", [P, CT, TAPS])
        cb = sb("cb", [P, CT])
        dtb = sb("dtb", [P, H])
        negA = sb("negA", [P, H])
        dskip = sb("dskip", [P, H])
        nw = sb("nw", [P, XT])
        Win = sb("Win", [P, 2, KD, DP], F16)
        Wout = sb("Wout", [P, 2, XT, D], F16)
        Wup = sb("Wup", [P, KD, DE], F8)
        Wgate = sb("Wgate", [P, KD, DE], F8)
        Wdown = sb("Wdown", [P, ET, D], F8)
        wsc = sb("wsc", [P, 40])
        uTf = sb("uTf", [P, KD, T])
        uTs = sb("uTs", [P, 2, KD, T], F16)
        halo = sb("halo", [P, CT, HALO])
        BT = sb("BT", [P, T])
        CTt = sb("CTt", [P, T])
        Btok = sb("Btok", [P, NC, P])
        xtok = sb("xtok", [P, NC, DI])
        S = sb("S", [P, DI])
        x1 = sb("x1", [P, NC, D])
        x1T = sb("x1T", [P, 2, KD, T], F16)
        hid = sb("hid", [P, 2, EH, T], F16)
        dts = sb("dts", [P, 10, NC * H])
        a16 = sb("a16", [P, 2, NC * H], F16)
        dec = sb("dec", [P, 3, NC * H])
        sc = sb("sc", [P, 2, 16])
        st = sb("st", [P, 2, NC, 16])
        CBm = sb("CBm", [P, P])
        work = sb("work", [P, 10240])

        def cut(start, shape, dt=F32):
            n = 1
            for s in shape:
                n *= s
            words = n // (2 if dt == F16 else 1)
            v = work[:, start:start + words]
            if dt != F32:
                v = v.bitcast(dt)
            if len(shape) == 2:
                v = v.rearrange("p (a b) -> p a b", a=shape[0])
            return v, start + words

        at = 0
        pre, at = cut(at, [2, HALO + 1 + T])
        acc, at = cut(at, [4, T])
        tnh, at = cut(at, [2, T])
        fth, at = cut(at, [2, T])
        fp, at = cut(at, [2, T])
        fh, at = cut(at, [2, T])
        at = 0
        Lm, at = cut(at, [H, P])
        am, at = cut(at, [4, DI], F16)
        xdt, at = cut(at, [DI])
        xs, at = cut(at, [DI])
        y, at = cut(at, [DI])
        yd, at = cut(at, [DI])
        zs, at = cut(at, [DI])
        yT, at = cut(at, [2 * XT, P], F16)
        assert at <= 10240
        Wstage, _ = cut(0, [KD, DP])

        psM = [ctx.enter_context(nc.psum_tensor(f"psM{i}", [P, T], F32)) for i in range(4)]
        psF = [ctx.enter_context(nc.psum_tensor(f"psF{i}", [P, T], F32)) for i in range(4)]

        sems = []

        def line(eng, name, step=1):
            s = ctx.enter_context(nc.semaphore(name))
            sems.append(s)
            return Line(clock, eng, s, step)

        PE = line(nc.tensor, "pe_done")
        V = line(nc.vector, "dve_done")
        A = line(nc.scalar, "act_done")
        G = line(nc.gpsimd, "pool_done")
        LU = line(nc.sync, "uT_loaded", 16)
        LR = [line(nc.sync, f"u_loaded{c}", 16) for c in range(NC)]
        ST = [line(nc.sync, f"y_stored{c}", 16) for c in range(NC)]
        LW = [line(nc.sync, f"w_loaded{i}", 16) for i in range(4)]
        SP = Line(clock, nc.sync, ctx.enter_context(nc.semaphore("sp_unused")))

        def barrier():
            for ln in [LU, *LR, *ST, *LW]:
                SP.wait(ln.now())
            nums = sorted(s.num for s in sems)
            assert nums == list(range(nums[0], nums[0] + len(nums)))
            nc.all_engine_barrier(sems_to_clear=range(nums[0], nums[-1] + 1))
            clock.turn()

        psM_turn, psF_turn = cycle(range(4)), cycle(range(4))
        pre_turn, acc_turn, tnh_turn, am_turn = cycle(range(2)), cycle(range(4)), cycle(range(2)), cycle(range(2))
        fth_turn, fp_turn, fh_turn, stage_turn = cycle(range(2)), cycle(range(2)), cycle(range(2)), cycle(range(2))
        psM_read, psF_read = [None] * 4, [None] * 4
        pre_read, acc_read, tnh_read, am_read = [None] * 2, [None] * 4, [None] * 2, [None] * 2
        fth_read, fp_read, fh_read, stage_read = [None] * 2, [None] * 2, [None] * 2, [None] * 2

        IN_INV, OUT_INV, UP_T, FS = (wsc[:, i:i + 1] for i in range(4))
        thr = [wsc[:, 4 + i:5 + i] for i in range(3)]
        nthr = [wsc[:, 7 + i:8 + i] for i in range(3)]
        tmp = [wsc[:, 10 + i:11 + i] for i in range(8)]
        sums = wsc[:, 20:20 + 12]
        tot3 = wsc[:, 32:35]
        sum3 = wsc[:, 35:38]

        uT_v = uT.rearrange("(k p) (t n) -> p k t n", p=P, n=T)
        u_v = u.rearrange("b (h c p) d -> p (b h) c d", p=P, c=NC)
        out_v = out.rearrange("b (h c p) d -> p (b h) c d", p=P, c=NC)

        mk = {}

        def load_uT(t, *after):
            LU.wait(*after)
            mk["uT"] = LU.did(nc.sync.dma_start(uTf[:, :, :], uT_v[:, :, t, :]))

        def absmax_scale(src, top, out_inv, col):
            m = V.did(nc.vector.tensor_reduce(tmp[col], src, AX.X, ALU.max, apply_absolute_value=True))
            G.wait(m)
            m = G.did(nc.gpsimd.partition_all_reduce(tmp[col + 1], tmp[col], P, RED.max))
            V.wait(m)
            m = V.did(nc.vector.tensor_scalar(tmp[col + 1], tmp[col + 1], TINY, None, ALU.max))
            V.wait(m)
            V.did(nc.vector.tensor_scalar(out_inv, tmp[col + 1], 1.0 / top, None, ALU.mult))
            m = V.did(nc.vector.reciprocal(tmp[col], tmp[col + 1]))
            V.wait(m)
            return V.did(nc.vector.tensor_scalar(tmp[col], tmp[col], top, None, ALU.mult))

        def split(hi, lo, src, scale, after):
            A.wait(after)
            h = A.did(nc.scalar.activation(hi, src, ACT.Copy, scale=scale))
            V.wait(h, after)
            return h, V.did(nc.vector.scalar_tensor_tensor(lo, src, scale, hi, ALU.mult, ALU.subtract))

        def setup():
            for k in range(KD):
                mW = LW[0].did(nc.sync.dma_start(Wstage[:, k, :], W_inT.rearrange("(k p) n -> p k n", p=P)[:, k, :]))
            load_uT(0)
            stageO = xtok[:, :, :].rearrange("p c d -> p (c d)").rearrange("p (x d) -> p x d", x=XT)
            small = [
                (cw[:, :, :], conv_w.rearrange("(c p) w -> p c w", p=P)),
                (cb[:, :], conv_b.rearrange("(c p) -> p c", p=P)),
                (nw[:, :], norm_w.rearrange("(c p) -> p c", p=P)),
                (dtb[:, :], dt_bias.partition_broadcast(P)),
                (negA[:, :], A_log.partition_broadcast(P)),
                (dskip[:, :], Dp.partition_broadcast(P)),
            ]
            with nc.allow_non_contiguous_dma("small parameters"):
                for dst, src in small:
                    mS = LW[1].did(nc.sync.dma_start(dst, src))
            mO = LW[1].did(nc.sync.dma_start(stageO, W_outT.rearrange("(x p) d -> p x d", p=P)))
            for c in range(NC):
                mk["res", c] = LR[c].did(nc.sync.dma_start(x1[:, c, :], u_v[:, 0, c, :]))

            m = G.did(nc.gpsimd.memset(ones[:, :], 1.0))
            G.did(nc.gpsimd.memset(minus_half[:, :], -0.5))
            G.wait(m)
            G.did(nc.gpsimd.affine_select(out=ident[:, :], in_=ones[:, :], compare_op=ALU.is_equal, fill=0.0,
                                          base=0, pattern=[[-1, P]], channel_multiplier=1))
            G.did(nc.gpsimd.affine_select(out=tri_le[:, :], in_=ones[:, :], compare_op=ALU.is_ge, fill=0.0,
                                          base=0, pattern=[[1, P]], channel_multiplier=-1))
            m = G.did(nc.gpsimd.affine_select(out=tri_gt[:, :], in_=ones[:, :], compare_op=ALU.is_gt, fill=0.0,
                                              base=0, pattern=[[-1, P]], channel_multiplier=1))
            G.wait(m)
            G.did(nc.gpsimd.tensor_copy(tri_le16[:, :], tri_le[:, :]))
            mk["const"] = G.did(nc.gpsimd.tensor_copy(tri_gt16[:, :], tri_gt[:, :]))

            V.wait(mW)
            r = absmax_scale(Wstage.rearrange("p k n -> p (k n)"), W_TOP, IN_INV, 0)
            for k in range(KD):
                split(Win[:, 0, k, :], Win[:, 1, k, :], Wstage[:, k, :], tmp[0], r)
            mk["Win"] = [A.now(), V.now()]
            mk["phase"] = [A.now(), V.now()]
            V.wait(mS, mO)
            V.did(nc.vector.tensor_scalar(cw[:, :, :], cw[:, :, :], 0.5, None, ALU.mult))
            mk["cb"] = V.did(nc.vector.tensor_scalar(cb[:, :], cb[:, :], 0.5, None, ALU.mult))
            A.wait(mS, mO)
            m = A.did(nc.scalar.activation(negA[:, :], negA[:, :], ACT.Exp))
            V.wait(m)
            mk["negA"] = V.did(nc.vector.tensor_scalar(negA[:, :], negA[:, :], -1.0, None, ALU.mult))
            for x in range(XT):
                m = V.did(nc.vector.tensor_scalar(stageO[:, x, :], stageO[:, x, :], nw[:, x:x + 1], None, ALU.mult))
            V.wait(m)
            r = absmax_scale(stageO.rearrange("p x d -> p (x d)"), W_TOP * NORM_GAIN, OUT_INV, 2)
            V.wait(r)
            r = V.did(nc.vector.tensor_scalar(tmp[2], tmp[2], 1.0 / NORM_GAIN, None, ALU.mult))
            m = split(Wout[:, 0, :, :].rearrange("p x d -> p (x d)"), Wout[:, 1, :, :].rearrange("p x d -> p (x d)"),
                      stageO.rearrange("p x d -> p (x d)"), tmp[2], r)
            mk["Wout"] = list(m)
            G.wait(*m)

        def ffn_weights():
            stage = hid[:, :, :, :].rearrange("p a e t -> p (a e t)").bitcast(F32).rearrange("p (s n) -> p s n", s=2)
            mats = [(W_upT, Wup[:, :, :].rearrange("p k n -> p (k n)"), KD),
                    (W_gateT, Wgate[:, :, :].rearrange("p k n -> p (k n)"), KD),
                    (W_downT, Wdown[:, :, :].rearrange("p k n -> p (k n)"), ET)]
            width = stage.shape[2]
            pieces = DE * D // P // width

            def load(mat, piece):
                s = next(stage_turn)
                LW[2 + s].wait(stage_read[s])
                src, _, k = mats[mat]
                per = k // pieces
                v = src.rearrange("(x k p) n -> x p k n", p=P, k=per)[piece]
                dst = stage[:, s, :].rearrange("p (k n) -> p k n", k=per)
                return s, LW[2 + s].did(nc.sync.dma_start(dst, v))

            for mat in range(3):
                for piece in range(pieces):
                    s, m = load(mat, piece)
                    A.wait(m)
                    n = mat * pieces + piece
                    stage_read[s] = A.did(nc.scalar.activation(stage[:, s, :], stage[:, s, :], ACT.Abs,
                                                               accum_out=sums[:, n:n + 1]))
                    yield
            V.wait(A.now())
            m = V.did(nc.vector.tensor_reduce(sum3, sums.rearrange("p (m n) -> p m n", m=3), AX.X, ALU.add))
            G.wait(m)
            m = G.did(nc.gpsimd.partition_all_reduce(tot3, sum3, P, RED.add))
            V.wait(m)
            m = V.did(nc.vector.tensor_scalar(tot3, tot3, 1.0 / (DE * D), QUANT_EPS, ALU.mult, ALU.add))
            V.wait(m)
            V.did(nc.vector.tensor_scalar(wsc[:, 4:7], tot3, 0.5, None, ALU.mult))
            V.did(nc.vector.tensor_scalar(wsc[:, 7:10], tot3, -0.5, None, ALU.mult))
            V.did(nc.vector.tensor_scalar(UP_T, tot3[:, 0:1], 0.5 / NORM_GAIN, None, ALU.mult))
            m = V.did(nc.vector.tensor_scalar(tmp[7], tot3[:, 0:1], tot3[:, 1:2], 1.0 / HID_GAIN, ALU.mult, ALU.mult))
            V.wait(m)
            m = V.did(nc.vector.tensor_scalar(FS, tmp[7], tot3[:, 2:3], None, ALU.mult))
            V.wait(m)
            yield
            for mat in range(3):
                for piece in range(pieces):
                    s, m = load(mat, piece)
                    V.wait(m)
                    dst = mats[mat][1][:, piece * width:(piece + 1) * width]
                    m = V.did(nc.vector.tensor_scalar(dst, stage[:, s, :], nthr[mat], None, ALU.is_lt,
                                                       saturate=False))
                    V.wait(m)
                    m = V.did(nc.vector.scalar_tensor_tensor(dst, stage[:, s, :], thr[mat], dst,
                                                             ALU.is_gt, ALU.subtract, saturate=False))
                    stage_read[s] = m
                    yield
            mk["ffnW"] = V.now()

        def mixer_in(par, fresh, nxt):
            q = sc[:, par, :]
            umax, uall, su, comb, half = (q[:, i:i + 1] for i in range(5))
            w_last = q[:, 5:5 + CT]
            mk["comb", par] = None
            V.wait(mk["uT"])
            m = V.did(nc.vector.tensor_reduce(umax, uTf[:, :, :], AX.XY, ALU.max, apply_absolute_value=True))
            G.wait(m)
            m = G.did(nc.gpsimd.partition_all_reduce(uall, umax, P, RED.max))
            if fresh:
                G.wait(mk.get("S_read"), mk.get("S_done"))
                G.did(nc.gpsimd.memset(halo[:, :, :], 0.0))
                mk["S_done"] = G.did(nc.gpsimd.memset(S[:, :], 0.0))
                G.wait(mk["S_done"])
            V.wait(m)
            m = V.did(nc.vector.tensor_scalar(uall, uall, TINY, None, ALU.max))
            V.wait(m)
            m = V.did(nc.vector.reciprocal(su, uall))
            n = V.did(nc.vector.tensor_scalar(comb, uall, IN_INV, 1.0 / U_TOP, ALU.mult, ALU.mult))
            V.wait(m, n)
            m = V.did(nc.vector.tensor_scalar(su, su, U_TOP, None, ALU.mult))
            V.did(nc.vector.tensor_scalar(half, comb, 0.5, None, ALU.mult))
            n = V.did(nc.vector.tensor_scalar(w_last, cw[:, :, HALO], comb, None, ALU.mult))
            mk["comb", par] = n
            A.wait(mk.get("uTs_read"), m, n)
            V.wait(mk.get("uTs_read"), m)
            parts = []
            for k in range(0, KD, 2):
                flat = [uTs[:, i, k:k + 2, :].rearrange("p k t -> p (k t)") for i in range(2)]
                parts += split(flat[0], flat[1], uTf[:, k:k + 2, :].rearrange("p k t -> p (k t)"), su, m)
            mk["uTs"] = parts
            if nxt is not None:
                load_uT(nxt, *parts)
            yield

            def project(bank, cols, tok, n, width, channels_out):
                for k in range(KD):
                    for wi, ui in ((0, 0), (0, 1), (1, 0)):
                        w = Win[:, wi, k, cols:cols + width]
                        x = uTs[:, ui, k, tok:tok + n]
                        i = nc.tensor.matmul(bank, w if channels_out else x, x if channels_out else w,
                                             start=(k == 0 and wi == ui), stop=(k == KD - 1 and wi == 1))
                return PE.did(i)

            def project_dt():
                PE.wait(mk["uTs"])
                b = next(psM_turn)
                bank = psM[b]
                PE.wait(psM_read[b])
                for c in range(NC):
                    p = project(bank[:, c * H:(c + 1) * H], DI + CD, c * P, P, H, False)
                d = [dts[:, i, :] for i in range(10)]

                def bc(v):
                    return v.unsqueeze(1).broadcast_to([P, NC, H])

                def by_chunk(v):
                    return v.rearrange("p (c h) -> p c h", c=NC)

                raw, low, e, s2, q2, pl, dt, a, dldt, s_ = d

                def step(ins):
                    V.wait(V.did(ins))
                v = nc.vector
                V.wait(p, mk["negA"], mk.get("dt_read"), mk["comb", par])
                step(v.scalar_tensor_tensor(by_chunk(raw), by_chunk(bank[:, 0:NC * H]), comb, bc(dtb[:, :]),
                                            ALU.mult, ALU.add))
                psM_read[b] = [V.now()]
                step(v.tensor_scalar(low, raw, -1.0, None, ALU.mult))
                step(v.tensor_tensor(low, low, raw, ALU.min))
                A.wait(V.now())
                V.wait(A.did(nc.scalar.activation(e, low, ACT.Exp)))
                step(v.tensor_scalar(s_, e, 2.0, None, ALU.add))
                step(v.reciprocal(s_, s_))
                step(v.tensor_tensor(s_, s_, e, ALU.mult))
                step(v.tensor_tensor(q2, s_, s_, ALU.mult))
                step(v.tensor_scalar(pl, q2, 1.0 / 15, None, ALU.mult))
                for odd in (13, 11, 9, 7, 5, 3):
                    step(v.scalar_tensor_tensor(pl, pl, 1.0 / odd, q2, ALU.add, ALU.mult))
                step(v.scalar_tensor_tensor(pl, pl, 1.0, s_, ALU.add, ALU.mult))
                step(v.tensor_scalar(pl, pl, 2.0, None, ALU.mult))
                step(v.scalar_tensor_tensor(dt, raw, 0.0, pl, ALU.max, ALU.add))
                step(v.tensor_tensor(by_chunk(a), by_chunk(dt), bc(negA[:, :]), ALU.mult))
                step(v.tensor_scalar(low, a, A_GAIN, A_FLOOR, ALU.mult, ALU.max))
                V.wait(mk.get("a16_read"))
                step(v.tensor_copy(a16[:, 0, :], low))
                step(v.tensor_tensor(a16[:, 1, :], low, a16[:, 0, :], ALU.subtract))
                mk["a16"] = V.now()

                PE.wait(mk["a16"], mk["const"])
                b = next(psM_turn)
                bank = psM[b]
                PE.wait(psM_read[b])
                for i, w in enumerate((tri_le, tri_gt, ones)):
                    p = PE.did(nc.tensor.matmul(bank[:, i * NC * H:(i + 1) * NC * H], w[:, :], a,
                                                start=True, stop=True))
                A.wait(p, mk.get("dt_read"))
                m = A.did(nc.scalar.activation(dec[:, :, :].rearrange("p s n -> p (s n)"), bank[:, 0:3 * NC * H],
                                               ACT.Exp))
                psM_read[b] = [m]
                V.wait(m)
                mk["dec"] = [m, V.did(v.tensor_tensor(dldt, dec[:, 1, :], dt, ALU.mult))]

            order = [XT, XT + 1] + list(range(XT))
            live = {}
            LAST = len(order) + 3
            for n in range(LAST):
                if n < len(order):
                    ct = order[n]
                    PE.wait(mk["uTs"], mk["Win"])
                    b = next(psM_turn)
                    bank = psM[b]
                    PE.wait(psM_read[b])
                    p = project(bank[:, :], DI + ct * P, 0, T, P, True)
                    s = next(pre_turn)
                    A.wait(pre_read[s])
                    G.wait(mk.get(("halo", ct)), pre_read[s])
                    h = G.did(nc.gpsimd.tensor_copy(pre[:, s, 1:1 + HALO], halo[:, ct, :]))
                    A.wait(p, mk["comb", par])
                    m1 = A.did(nc.scalar.activation(pre[:, s, 1 + HALO:1 + HALO + T], bank[:, :], ACT.Copy, scale=comb))
                    r = next(acc_turn)
                    A.wait(acc_read[r])
                    A.wait(mk["cb"])
                    m2 = A.did(nc.scalar.activation(acc[:, r, :], bank[:, :], ACT.Identity,
                                                    scale=w_last[:, ct:ct + 1], bias=cb[:, ct:ct + 1]))
                    psM_read[b] = [m1, m2]
                    G.wait(m1, h)
                    mk["halo", ct] = G.did(nc.gpsimd.tensor_copy(halo[:, ct, :], pre[:, s, 1 + T:1 + T + HALO]))
                    live[n] = dict(s=s, r=r, m=[h, m1, m2], halo=mk["halo", ct])
                if 0 <= n - 1 < len(order):
                    ct, w = order[n - 1], live[n - 1]
                    V.wait(w["m"])
                    for tap in range(HALO - 1, -1, -1):
                        m = V.did(nc.vector.scalar_tensor_tensor(acc[:, w["r"], :], pre[:, w["s"], 1 + tap:1 + tap + T],
                                                                 cw[:, ct, tap:tap + 1], acc[:, w["r"], :],
                                                                 ALU.mult, ALU.add))
                        V.wait(m)
                    pre_read[w["s"]] = [m, w["halo"]]
                    w["t"] = next(tnh_turn)
                    A.wait(tnh_read[w["t"]])
                    A.wait(m)
                    w["tanh"] = A.did(nc.scalar.activation(tnh[:, w["t"], :], acc[:, w["r"], :], ACT.Tanh))
                if 0 <= n - 2 < len(order):
                    ct, w = order[n - 2], live[n - 2]
                    if ct == XT:
                        dst = BT[:, :]
                        V.wait(mk.get("BT_read"))
                    elif ct == XT + 1:
                        dst = CTt[:, :]
                        V.wait(mk.get("CT_read"))
                    else:
                        dst = acc[:, w["r"], :]
                    V.wait(w["tanh"])
                    m = V.did(nc.vector.scalar_tensor_tensor(dst, tnh[:, w["t"], :], 1.0, acc[:, w["r"], :],
                                                             ALU.add, ALU.mult))
                    tnh_read[w["t"]] = [m]
                    acc_read[w["r"]] = [m]
                    w["silu"] = m
                    if ct >= XT:
                        mk["BT" if ct == XT else "CT"] = m
                if 0 <= n - 3 < len(order):
                    ct, w = order[n - 3], live[n - 3]
                    if ct != XT + 1:
                        PE.wait(w["silu"], mk["const"])
                        src = BT[:, :] if ct == XT else acc[:, w["r"], :]
                        b = next(psM_turn)
                        bank = psM[b]
                        PE.wait(psM_read[b])
                        for c in range(NC):
                            i = nc.tensor.transpose(bank[:, c * P:(c + 1) * P], src[:, c * P:(c + 1) * P], ident[:, :])
                        p = PE.did(i)
                        if ct != XT:
                            acc_read[w["r"]] = [p]
                        dst = Btok[:, :, :] if ct == XT else xtok[:, :, ct * P:(ct + 1) * P]
                        A.wait(p, mk.get("Btok_read") if ct == XT else mk.get("xtok_read"))
                        m = A.did(nc.scalar.activation(dst, bank[:, :].rearrange("p (c n) -> p c n", c=NC), ACT.Copy))
                        psM_read[b] = [m]
                        mk["Btok" if ct == XT else "xtok"] = m
                if n == 2:
                    project_dt()
                yield
            mk["project"] = project

        def end_phase():
            marks = [PE.now(), V.now(), A.now(), G.now()]
            for ln in (V, A, G):
                ln.wait(marks)

        def heads(v, n):
            return v.rearrange("p (h d) -> p h d", h=n)

        def front(c, par):
            half = sc[:, par, 4:5]
            ch = slice(c * H, (c + 1) * H)
            tok = slice(c * P, (c + 1) * P)
            PE.wait(mk["BT"], mk["CT"])
            b = next(psM_turn)
            bank = psM[b]
            PE.wait(psM_read[b])
            p = PE.did(nc.tensor.matmul(bank[:, 0:P], BT[:, tok], CTt[:, tok], start=True, stop=True))
            mk["BT_read"] = p
            V.wait(p, mk["const"])
            cbm = V.did(nc.vector.tensor_tensor(CBm[:, :], bank[:, 0:P], tri_le[:, :], ALU.mult))
            psM_read[b] = [cbm]
            HG = DI // P
            masked = []
            for g in range(H // HG):
                s = next(am_turn)
                G.wait(am_read[s])
                G.wait(mk["a16"])
                for part in range(2):
                    av = a16[:, part, c * H + g * HG:c * H + (g + 1) * HG]
                    m = G.did(nc.gpsimd.tensor_tensor(am[:, 2 * s + part, :].rearrange("p (h i) -> p h i", h=HG),
                                                      av.unsqueeze(2).broadcast_to([P, HG, P]),
                                                      tri_le16[:, :].unsqueeze(1).broadcast_to([P, HG, P]), ALU.mult))
                masked.append((s, m))
                yield
            V.wait(mk["xtok"], mk["dec"], mk.get("xdt_read"))
            mk["xdt"] = V.did(nc.vector.tensor_tensor(heads(xdt, H), heads(xtok[:, c, :], H),
                                                      dts[:, 6, ch].unsqueeze(2).broadcast_to([P, H, HD]), ALU.mult))
            G.wait(mk["xtok"], mk["dec"], mk.get("xs_read"), mk.get("yd_read"))
            mk["xs"] = G.did(nc.gpsimd.tensor_tensor(heads(xs, H), heads(xtok[:, c, :], H),
                                                     dts[:, 8, ch].unsqueeze(2).broadcast_to([P, H, HD]), ALU.mult))
            mk["yd"] = G.did(nc.gpsimd.tensor_tensor(heads(yd, H), heads(xtok[:, c, :], H),
                                                     dskip[:, :].unsqueeze(2).broadcast_to([P, H, HD]), ALU.mult))
            for w in range(ZW):
                PE.wait(mk["uTs"])
                b = next(psM_turn)
                bank = psM[b]
                PE.wait(psM_read[b])
                p = mk["project"](bank[:, :], w * T, c * P, P, T, False)
                mk["uTs_read"] = p
                zw = zs[:, w * T:(w + 1) * T]
                A.wait(p, mk.get("zs_read"))
                m = A.did(nc.scalar.activation(zw, bank[:, :], ACT.Tanh, scale=half))
                V.wait(m)
                mk["zs"] = V.did(nc.vector.scalar_tensor_tensor(zw, zw, 1.0, bank[:, :], ALU.add, ALU.mult))
                psM_read[b] = [m, mk["zs"]]
                yield
            for r in range(H // HQ):
                s, m = masked[r * HQ // HG]
                PE.wait(m)
                b = next(psM_turn)
                bank = psM[b]
                PE.wait(psM_read[b])
                lo = (r * HQ % HG) * P
                for part in range(2):
                    ins = nc.tensor.matmul(bank[:, :], tri_gt16[:, :], am[:, 2 * s + part, lo:lo + T],
                                           start=part == 0, stop=part == 1)
                p = PE.did(ins)
                am_read[s] = [p]
                Lq = Lm[:, r * HQ:(r + 1) * HQ, :]
                A.wait(p, mk.get("L_read"))
                e = A.did(nc.scalar.activation(Lq, bank[:, :].rearrange("p (h i) -> p h i", h=HQ), ACT.Exp,
                                               scale=1.0 / A_GAIN))
                psM_read[b] = [e]
                V.wait(e, cbm)
                mk["L", r] = V.did(nc.vector.tensor_tensor(Lq, Lq, CBm[:, :].unsqueeze(1).broadcast_to([P, HQ, P]),
                                                           ALU.mult))
                if r % 2:
                    yield

        def middle(c, par):
            half = sc[:, par, 4:5]
            ch = slice(c * H, (c + 1) * H)
            tok = slice(c * P, (c + 1) * P)
            HG = H // 2
            for w in range(2):
                cols = slice(w * T, (w + 1) * T)
                hs = slice(w * HG, (w + 1) * HG)
                PE.wait(mk["S_done"], mk["CT"])
                b = next(psM_turn)
                bank = psM[b]
                PE.wait(psM_read[b])
                p = PE.did(nc.tensor.matmul(bank[:, :], CTt[:, tok], S[:, cols], start=True, stop=True))
                mk["S_read"] = mk["CT_read"] = p
                V.wait(p, mk.get("y_read"))
                m = V.did(nc.vector.tensor_tensor(heads(y[:, cols], HG), heads(bank[:, :], HG),
                                                  dec[:, 0, ch][:, hs].unsqueeze(2).broadcast_to([P, HG, HD]), ALU.mult))
                psM_read[b] = [m]
                V.wait(m, mk["yd"])
                mk["yoff", w] = V.did(nc.vector.tensor_tensor(y[:, cols], y[:, cols], yd[:, cols], ALU.add))
            mk["yd_read"] = mk["yoff", 1]
            yield
            G.wait(mk["S_read"], mk["S_done"], mk["dec"])
            sd = G.did(nc.gpsimd.tensor_tensor(heads(S[:, :], H), heads(S[:, :], H),
                                               dec[:, 2, ch].unsqueeze(2).broadcast_to([P, H, HD]), ALU.mult))
            for w in range(2):
                cols = slice(w * T, (w + 1) * T)
                PE.wait(mk["xs"], mk["Btok"])
                b = next(psM_turn)
                bank = psM[b]
                PE.wait(psM_read[b])
                p = PE.did(nc.tensor.matmul(bank[:, :], Btok[:, c, :], xs[:, cols], start=True, stop=True))
                mk["xs_read"] = mk["Btok_read"] = p
                V.wait(p, sd)
                mk["S_done"] = V.did(nc.vector.tensor_tensor(S[:, cols], S[:, cols], bank[:, :], ALU.add))
                psM_read[b] = [mk["S_done"]]
            yield
            for w in range(2):
                cols = slice(w * T, (w + 1) * T)
                b = next(psM_turn)
                bank = psM[b]
                PE.wait(psM_read[b])
                for h in range(w * HG, (w + 1) * HG):
                    PE.wait(mk["L", h // HQ], mk["xdt"])
                    ins = nc.tensor.matmul(bank[:, (h - w * HG) * HD:(h - w * HG + 1) * HD], Lm[:, h, :],
                                           xdt[:, h * HD:(h + 1) * HD], start=True, stop=True)
                p = PE.did(ins)
                mk["L_read"] = mk["xdt_read"] = p
                V.wait(p, mk["yoff", w])
                m = V.did(nc.vector.tensor_tensor(y[:, cols], y[:, cols], bank[:, :], ALU.add))
                psM_read[b] = [m]
                V.wait(m, mk["zs"])
                mk["y"] = V.did(nc.vector.scalar_tensor_tensor(y[:, cols], y[:, cols], half, zs[:, cols],
                                                               ALU.mult, ALU.mult))
                yield
            ss, r = st[:, par, c, 0:1], st[:, par, c, 1:2]
            A.wait(mk["y"])
            m = A.did(nc.scalar.activation(zs, y, ACT.Square, accum_out=ss))
            mk["zs_read"] = m
            G.wait(m)
            m = G.did(nc.gpsimd.tensor_scalar(r, ss, 1.0 / DI, RMS_EPS, ALU.mult, ALU.add))
            G.wait(m)
            m = G.did(nc.gpsimd.tensor_tensor(r, r, minus_half[:, :], ALU.pow))
            A.wait(m)
            mk["yn"] = A.did(nc.scalar.activation(y, y, ACT.Copy, scale=r))
            mk["xtok_read"] = [G.now(), V.now()]
            mk["dt_read"] = [G.now(), V.now()]
            mk["a16_read"] = G.now()
            yield

        def layernorm(c, par, col, h):
            row = x1[:, c, :]
            s6, mv, r = st[:, par, c, col:col + 6], st[:, par, c, 14:16], st[:, par, c, 13:14]
            V.wait(h)
            m = V.did(nc.vector.bn_stats(s6, row))
            V.wait(m)
            m = V.did(nc.vector.bn_aggr(mv, s6))
            G.wait(m)
            m = G.did(nc.gpsimd.tensor_scalar(r, mv[:, 1:2], LN_EPS, None, ALU.add))
            G.wait(m)
            m = G.did(nc.gpsimd.tensor_tensor(r, r, minus_half[:, :], ALU.pow))
            V.wait(m)
            return V.did(nc.vector.tensor_scalar(row, row, mv[:, 0:1], r, ALU.subtract, ALU.mult))

        def back(c, par):
            PE.wait(mk["yn"])
            for w in range(2):
                b = next(psM_turn)
                bank = psM[b]
                PE.wait(psM_read[b])
                for x in range(4):
                    ins = nc.tensor.transpose(bank[:, x * P:(x + 1) * P], y[:, (4 * w + x) * P:(4 * w + x + 1) * P],
                                              ident[:, :])
                p = PE.did(ins)
                mk["y_read"] = p
                hi, lo = (yT[:, i * XT + 4 * w:i * XT + 4 * w + 4, :].rearrange("p x n -> p (x n)") for i in range(2))
                A.wait(p, mk.get("yT_read"))
                m = A.did(nc.scalar.activation(hi, bank[:, :], ACT.Copy, scale=NORM_GAIN))
                V.wait(m, p, mk.get("yT_read"))
                mk["yT", w] = V.did(nc.vector.scalar_tensor_tensor(lo, bank[:, :], NORM_GAIN, hi,
                                                                   ALU.mult, ALU.subtract))
                psM_read[b] = [m, mk["yT", w]]
            yield
            b = next(psM_turn)
            bank = psM[b]
            PE.wait(psM_read[b])
            PE.wait(mk["Wout"])
            for x in range(XT):
                PE.wait(mk["yT", x // 4])
                for yi, wi in ((0, 0), (0, 1), (1, 0)):
                    ins = nc.tensor.matmul(bank[:, :], yT[:, yi * XT + x, :], Wout[:, wi, x, :],
                                           start=(x == 0 and yi == wi), stop=(x == XT - 1 and yi == 1))
            p = PE.did(ins)
            mk["yT_read"] = p
            yield
            V.wait(p, mk["res", c])
            h = V.did(nc.vector.scalar_tensor_tensor(x1[:, c, :], bank[:, :], OUT_INV, x1[:, c, :], ALU.mult, ALU.add))
            psM_read[b] = [h]
            n = layernorm(c, par, 2, h)
            yield
            PE.wait(n)
            b = next(psM_turn)
            bank = psM[b]
            PE.wait(psM_read[b])
            for k in range(KD):
                ins = nc.tensor.transpose(bank[:, k * P:(k + 1) * P], x1[:, c, k * P:(k + 1) * P], ident[:, :])
            p = PE.did(ins)
            hi, lo = (x1T[:, i, :, c * P:(c + 1) * P] for i in range(2))
            bv = bank[:, :].rearrange("p (k n) -> p k n", k=KD)
            A.wait(p, mk.get("x1T_read"))
            m = A.did(nc.scalar.activation(hi, bv, ACT.Copy, scale=NORM_GAIN))
            V.wait(m, p, mk.get("x1T_read"))
            l = V.did(nc.vector.scalar_tensor_tensor(lo, bv, NORM_GAIN, hi, ALU.mult, ALU.subtract))
            psM_read[b] = [m, l]
            mk["x1T_new", c] = [m, l]
            mk["x1", c] = n
            yield

        def ffn_up(half):
            live = {}
            for n in range(EH + 1):
                if n < EH:
                    e = half * EH + n
                    PE.wait(mk["x1T"], mk.get("ffnW"))
                    ps = []
                    for Wm in (Wup, Wgate):
                        b = next(psF_turn)
                        bank = psF[b]
                        PE.wait(psF_read[b])
                        for k in range(KD):
                            for i in range(2):
                                ins = nc.tensor.matmul(bank[:, :], Wm[:, k, e * P:(e + 1) * P], x1T[:, i, k, :],
                                                       start=(k == 0 and i == 0), stop=(k == KD - 1 and i == 1))
                        ps.append((bank, b, PE.did(ins)))
                    mk["x1T_read"] = ps[1][2]
                    (Ub, ub, up), (Gb, gb, gp) = ps
                    t = next(fth_turn)
                    A.wait(fth_read[t])
                    A.wait(up)
                    m = A.did(nc.scalar.activation(fth[:, t, :], Ub[:, :], ACT.Tanh, scale=UP_T))
                    live[n] = (t, m, Ub, ub, Gb, gb, gp)
                if n >= 1:
                    t, m, Ub, ub, Gb, gb, gp = live[n - 1]
                    q = next(fp_turn)
                    V.wait(fp_read[q])
                    V.wait(m)
                    m = V.did(nc.vector.scalar_tensor_tensor(fp[:, q, :], fth[:, t, :], 1.0, Ub[:, :],
                                                             ALU.add, ALU.mult))
                    fth_read[t] = [m]
                    psF_read[ub] = [m]
                    f = next(fh_turn)
                    V.wait(fh_read[f])
                    V.wait(m, gp)
                    m = V.did(nc.vector.scalar_tensor_tensor(fh[:, f, :], fp[:, q, :],
                                                             0.5 * HID_GAIN / NORM_GAIN ** 2, Gb[:, :],
                                                             ALU.mult, ALU.mult))
                    fp_read[q] = [m]
                    psF_read[gb] = [m]
                    A.wait(m, mk.get("hid_read"))
                    h = A.did(nc.scalar.activation(hid[:, 0, n - 1, :], fh[:, f, :], ACT.Copy))
                    V.wait(h, m, mk.get("hid_read"))
                    l = V.did(nc.vector.tensor_tensor(hid[:, 1, n - 1, :], fh[:, f, :], hid[:, 0, n - 1, :],
                                                      ALU.subtract))
                    fh_read[f] = [h, l]
                    mk["hid", n - 1] = [h, l]
                yield

        def ffn_down(half, c):
            b = next(psF_turn)
            bank = psF[b]
            PE.wait(psF_read[b])
            for n in range(EH):
                PE.wait(mk["hid", n])
                for i in range(2):
                    ins = nc.tensor.matmul(bank[:, :], hid[:, i, n, c * P:(c + 1) * P], Wdown[:, half * EH + n, :],
                                           start=(n == 0 and i == 0), stop=(n == EH - 1 and i == 1))
            p = PE.did(ins)
            mk["hid_read"] = p
            V.wait(p, mk["x1", c])
            m = V.did(nc.vector.scalar_tensor_tensor(x1[:, c, :], bank[:, :], FS, x1[:, c, :], ALU.mult, ALU.add))
            psF_read[b] = [m]
            mk["x1", c] = m

        def ffn_end(c, par, t, nxt):
            ffn_down(1, c)
            n = layernorm(c, 1 - par, 2, mk["x1", c])
            ST[c].wait(n)
            s = ST[c].did(nc.sync.dma_start(out_v[:, t, c, :], x1[:, c, :]))
            if nxt is not None:
                LR[c].wait(s)
                mk["res", c] = LR[c].did(nc.sync.dma_start(x1[:, c, :], u_v[:, nxt, c, :]))

        def ffn_first(half_steps=None):
            mk["x1T"] = [mk.get(("x1T_new", c)) for c in range(NC)]
            yield from ffn_up(0)
            for c in range(NC):
                ffn_down(0, c)
                yield
            yield from ffn_up(1)

        def run(*gens):
            for g in gens:
                for _ in g:
                    pass

        def phase2(par, ffn_t, nxt):
            def tail(c):
                if ffn_t is not None:
                    ffn_end(c, par, ffn_t, nxt)
            run(front(0, par))
            tail(0)
            for c in range(NC):
                run(middle(c, par))
                if c + 1 < NC:
                    run(front(c + 1, par))
                    tail(c + 1)
                run(back(c, par))

        def tile(par, mixer_t, prefetch_t, ffn_t):
            drain((mixer_in(par, par == 0, prefetch_t), 14), (ffn_first(), 22))
            end_phase()
            phase2(par, ffn_t, mixer_t)
            end_phase()

        setup()
        A.wait(mk["phase"])
        G.wait(mk["phase"])
        drain((mixer_in(0, True, 1), 14), (ffn_weights(), 25))
        end_phase()
        phase2(0, None, None)
        barrier()
        with nc.Fori(0, NT // 2 - 1) as i:
            tile(1, 2 * i + 1, 2 * i + 2, 2 * i)
            tile(0, 2 * i + 2, 2 * i + 3, 2 * i + 1)
            barrier()
        tile(1, NT - 1, None, NT - 2)
        run(ffn_first())
        for c in range(NC):
            ffn_end(c, 0, NT - 1, None)
        for c in range(NC):
            SP.wait(ST[c].now())


_INS = ["u", "uT", "W_inT", "conv_w", "conv_b", "dt_bias", "A_log", "Dp", "norm_w", "W_outT", "W_upT", "W_gateT",
        "W_downT"]


def kernel(**inputs):
    import numpy as np
    import concourse.bacc as bacc
    from concourse import mybir as _mybir
    from concourse.bass_utils import run_bass_kernel_spmd

    g = {k: np.asarray(v) for k, v in inputs.items()}
    u = g["L0_attn_u"]
    rows = {
        "u": u,
        "uT": u.reshape(-1, u.shape[-1]).T,
        "W_inT": g["L0_attn_W_in"].T,
        "conv_w": g["L0_attn_conv_w"],
        "conv_b": g["L0_attn_conv_b"],
        "dt_bias": g["L0_attn_dt_bias"],
        "A_log": g["L0_attn_A_log"],
        "Dp": g["L0_attn_Dp"],
        "norm_w": g["L0_attn_norm_w"],
        "W_outT": g["L0_attn_W_out"].T,
        "W_upT": g["L0_ffn_W_up"].T,
        "W_gateT": g["L0_ffn_W_gate"].T,
        "W_downT": g["L0_ffn_W_down"].T,
    }
    nc = bacc.Bacc("TRN2", target_bir_lowering=False, num_devices=1)
    arrays, args = {}, []
    for name in _INS:
        a = np.ascontiguousarray(rows[name])
        arrays[f"in_{name}"] = a
        args.append(nc.dram_tensor(f"in_{name}", a.shape, _mybir.dt.from_np(a.dtype), kind="ExternalInput").ap())
    args.append(nc.dram_tensor("out_y", u.shape, _mybir.dt.from_np(u.dtype), kind="ExternalOutput").ap())
    build(nc, *args)
    r = run_bass_kernel_spmd(nc, [arrays], core_ids=[0])
    return r.results[0]["out_y"]
```

```python
from contextlib import ExitStack
from itertools import cycle

import concourse.bass as bass
from concourse import mybir

ALU = mybir.AluOpType
ACT = mybir.ActivationFunctionType
AX = mybir.AxisListType
F32 = mybir.dt.float32
F16 = mybir.dt.float16
F8 = mybir.dt.float8e4
RED = bass.bass_isa.ReduceOp

P = 128
U_TOP = 1024.0
W_TOP = 256.0
A_GAIN = 256.0
A_FLOOR = -60000.0
NORM_GAIN = 1024.0
HID_GAIN = 1.0 / 8.0
LN_EPS = 1e-5
RMS_EPS = 1e-5
QUANT_EPS = 1e-8
TINY = 1e-30


class Line:

    def __init__(self, clock, eng, sem, step=1):
        self.clock, self.eng, self.sem, self.step = clock, eng, sem, step
        self.count = 0
        self.seen = {}
        clock.lines.append(self)

    def did(self, ins):
        ins.then_inc(self.sem, self.step)
        self.count += self.step
        return (self.clock.epoch, self, self.count)

    def wait(self, *marks):
        for m in marks:
            if m is None:
                continue
            if isinstance(m, list):
                self.wait(*m)
                continue
            epoch, line, value = m
            if epoch == self.clock.epoch and self.seen.get(line.sem, 0) < value:
                self.eng.wait_ge(line.sem, value)
                self.seen[line.sem] = value

    def now(self):
        return (self.clock.epoch, self, self.count) if self.count else None


class Clock:
    def __init__(self):
        self.epoch = 0
        self.lines = []

    def turn(self):
        self.epoch += 1
        for line in self.lines:
            line.count = 0
            line.seen = {}


def drain(*steps):
    total = max(n for _, n in steps)
    done = [0] * len(steps)
    for k in range(1, total + 1):
        for i, (gen, n) in enumerate(steps):
            while done[i] < (k * n + total - 1) // total:
                next(gen, None)
                done[i] += 1


def build(nc, u, uT, W_inT, conv_w, conv_b, dt_bias, A_log, Dp, norm_w, W_outT, W_upT, W_gateT, W_downT, out):
    B, L, D = u.shape
    DI = W_outT.shape[0]
    H = Dp.shape[0]
    CD = conv_w.shape[0]
    NS = (CD - DI) // 2
    HD = DI // H
    DE = W_upT.shape[1]
    DP = W_inT.shape[1]
    TAPS = conv_w.shape[1]
    HALO = TAPS - 1
    T = 512
    NT = B * L // T
    NC = T // P
    KD = D // P
    CT = CD // P
    XT = DI // P
    ET = DE // P
    EH = ET // 2
    ZW = DI // T
    HB = T // HD
    HQ = T // P
    assert L == 2 * T and NS == P and DI % T == 0 and D == T and HD * 2 == P

    clock = Clock()
    with ExitStack() as ctx:
        def sb(name, shape, dt=F32):
            return ctx.enter_context(nc.sbuf_tensor(name, shape, dt))

        ident = sb("ident", [P, P])
        tri_le = sb("tri_le", [P, P])
        tri_gt = sb("tri_gt", [P, P])
        ones = sb("ones", [P, P])
        tri_le16 = sb("tri_le16", [P, P], F16)
        tri_gt16 = sb("tri_gt16", [P, P], F16)
        minus_half = sb("minus_half", [P, 1])
        cw = sb("cw", [P, CT, TAPS])
        cb = sb("cb", [P, CT])
        dtb = sb("dtb", [P, H])
        negA = sb("negA", [P, H])
        dskip = sb("dskip", [P, H])
        nw = sb("nw", [P, XT])
        Win = sb("Win", [P, 2, KD, DP], F16)
        Wout = sb("Wout", [P, 2, XT, D], F16)
        Wup = sb("Wup", [P, KD, DE], F8)
        Wgate = sb("Wgate", [P, KD, DE], F8)
        Wdown = sb("Wdown", [P, ET, D], F8)
        wsc = sb("wsc", [P, 40])
        uTf = sb("uTf", [P, KD, T])
        uTs = sb("uTs", [P, 2, KD, T], F16)
        halo = sb("halo", [P, CT, HALO])
        BT = sb("BT", [P, T])
        CTt = sb("CTt", [P, T])
        Btok = sb("Btok", [P, NC, P])
        xtok = sb("xtok", [P, NC, DI])
        S = sb("S", [P, DI])
        x1 = sb("x1", [P, NC, D])
        x1T = sb("x1T", [P, 2, KD, T], F16)
        hid = sb("hid", [P, 2, EH, T], F16)
        dts = sb("dts", [P, 10, NC * H])
        a16 = sb("a16", [P, 2, NC * H], F16)
        dec = sb("dec", [P, 3, NC * H])
        sc = sb("sc", [P, 2, 16])
        st = sb("st", [P, 2, NC, 16])
        CBm = sb("CBm", [P, P])
        WORK = 11272
        work = sb("work", [P, WORK])
        res = sb("res", [P, 2, D])

        def cut(start, shape, dt=F32):
            n = 1
            for s in shape:
                n *= s
            words = n // (2 if dt == F16 else 1)
            v = work[:, start:start + words]
            if dt != F32:
                v = v.bitcast(dt)
            if len(shape) == 2:
                v = v.rearrange("p (a b) -> p a b", a=shape[0])
            return v, start + words

        at = 0
        pre, at = cut(at, [2, HALO + 1 + T])
        acc, at = cut(at, [4, T])
        tnh, at = cut(at, [2, T])
        mixer_end = at
        fth, at = cut(at, [2, T])
        fp, at = cut(at, [2, T])
        fh, at = cut(at, [2, T])
        phase1_end = at
        at = 0
        am, at = cut(at, [4, DI], F16)
        xs, at = cut(at, [DI])
        yd, at = cut(at, [DI])
        assert at <= mixer_end
        xdt, at = cut(at, [DI])
        Lm, at = cut(at, [H, P])
        at = max(at, phase1_end)
        y, at = cut(at, [DI])
        zs2, at = cut(at, [2, DI])
        yT, at = cut(at, [2 * XT, P], F16)
        assert at <= WORK
        Wstage, _ = cut(0, [KD, DP])

        psM = [ctx.enter_context(nc.psum_tensor(f"psM{i}", [P, T], F32)) for i in range(4)]
        psF = [ctx.enter_context(nc.psum_tensor(f"psF{i}", [P, T], F32)) for i in range(4)]

        sems = []

        def line(eng, name, step=1):
            s = ctx.enter_context(nc.semaphore(name))
            sems.append(s)
            return Line(clock, eng, s, step)

        PE = line(nc.tensor, "pe_done")
        V = line(nc.vector, "dve_done")
        A = line(nc.scalar, "act_done")
        G = line(nc.gpsimd, "pool_done")
        LU = line(nc.sync, "uT_loaded", 16)
        LR = [line(nc.sync, f"u_loaded{c}", 16) for c in range(NC)]
        ST = [line(nc.sync, f"y_stored{c}", 16) for c in range(NC)]
        LS = line(nc.sync, "small_loaded", 16)
        LW = [line(nc.sync, f"w_loaded{i}", 16) for i in range(4)]
        SP = Line(clock, nc.sync, ctx.enter_context(nc.semaphore("sp_unused")))

        def barrier():
            for ln in [LU, LS, *LR, *ST, *LW]:
                SP.wait(ln.now())
            nums = sorted(s.num for s in sems)
            assert nums == list(range(nums[0], nums[0] + len(nums)))
            nc.all_engine_barrier(sems_to_clear=range(nums[0], nums[-1] + 1))
            clock.turn()

        psM_turn, psF_turn = cycle(range(4)), cycle(range(4))
        am_turn = cycle(range(2))
        fth_turn, fp_turn, fh_turn, stage_turn = cycle(range(2)), cycle(range(2)), cycle(range(2)), cycle(range(2))
        psM_read, psF_read = [None] * 4, [None] * 4
        pre_read, acc_read, tnh_read, am_read = [None] * 2, [None] * 4, [None] * 2, [None] * 2
        fth_read, fp_read, fh_read, stage_read = [None] * 2, [None] * 2, [None] * 2, [None] * 2

        IN_INV, OUT_INV, UP_T, FS = (wsc[:, i:i + 1] for i in range(4))
        thr = [wsc[:, 4 + i:5 + i] for i in range(3)]
        nthr = [wsc[:, 7 + i:8 + i] for i in range(3)]
        tmp = [wsc[:, 10 + i:11 + i] for i in range(8)]
        sums = wsc[:, 20:20 + 12]
        tot3 = wsc[:, 32:35]
        sum3 = wsc[:, 35:38]

        uT_v = uT.rearrange("(k p) (t n) -> p k t n", p=P, n=T)
        u_v = u.rearrange("b (h c p) d -> p (b h) c d", p=P, c=NC)
        out_v = out.rearrange("b (h c p) d -> p (b h) c d", p=P, c=NC)

        mk = {}

        def load_uT(t, *after):
            LU.wait(*after)
            mk["uT"] = LU.did(nc.sync.dma_start(uTf[:, :, :], uT_v[:, :, t, :]))

        def absmax_scale(src, top, out_inv, col):
            m = V.did(nc.vector.tensor_reduce(tmp[col], src, AX.X, ALU.max, apply_absolute_value=True))
            G.wait(m)
            m = G.did(nc.gpsimd.partition_all_reduce(tmp[col + 1], tmp[col], P, RED.max))
            V.wait(m)
            m = V.did(nc.vector.tensor_scalar(tmp[col + 1], tmp[col + 1], TINY, None, ALU.max))
            V.wait(m)
            V.did(nc.vector.tensor_scalar(out_inv, tmp[col + 1], 1.0 / top, None, ALU.mult))
            m = V.did(nc.vector.reciprocal(tmp[col], tmp[col + 1]))
            V.wait(m)
            return V.did(nc.vector.tensor_scalar(tmp[col], tmp[col], top, None, ALU.mult))

        def split(hi, lo, src, scale, after):
            A.wait(after)
            h = A.did(nc.scalar.activation(hi, src, ACT.Copy, scale=scale))
            V.wait(h, after)
            return h, V.did(nc.vector.scalar_tensor_tensor(lo, src, scale, hi, ALU.mult, ALU.subtract))

        def setup():
            for k in range(KD):
                mk["W_inT", k] = LW[k].did(nc.sync.dma_start(Wstage[:, k, :], W_inT.rearrange("(k p) n -> p k n", p=P)[:, k, :]))
            load_uT(0)
            small = [
                (cw[:, :, :], conv_w.rearrange("(c p) w -> p c w", p=P)),
                (cb[:, :], conv_b.rearrange("(c p) -> p c", p=P)),
                (nw[:, :], norm_w.rearrange("(c p) -> p c", p=P)),
                (dtb[:, :], dt_bias.partition_broadcast(P)),
                (negA[:, :], A_log.partition_broadcast(P)),
                (dskip[:, :], Dp.partition_broadcast(P)),
            ]
            with nc.allow_non_contiguous_dma("small parameters"):
                for dst, src in small:
                    mS = LS.did(nc.sync.dma_start(dst, src))
            for i in range(2):
                mk["W_outT"] = LS.did(nc.sync.dma_start(stageO[i], W_outT.rearrange("(i x p) d -> i p x d", p=P,
                                                                                    x=XH)[i]))

            m = G.did(nc.gpsimd.memset(ones[:, :], 1.0))
            G.did(nc.gpsimd.memset(minus_half[:, :], -0.5))
            G.wait(m)
            G.did(nc.gpsimd.affine_select(out=ident[:, :], in_=ones[:, :], compare_op=ALU.is_equal, fill=0.0,
                                          base=0, pattern=[[-1, P]], channel_multiplier=1))
            G.did(nc.gpsimd.affine_select(out=tri_le[:, :], in_=ones[:, :], compare_op=ALU.is_ge, fill=0.0,
                                          base=0, pattern=[[1, P]], channel_multiplier=-1))
            m = G.did(nc.gpsimd.affine_select(out=tri_gt[:, :], in_=ones[:, :], compare_op=ALU.is_gt, fill=0.0,
                                              base=0, pattern=[[-1, P]], channel_multiplier=1))
            G.wait(m)
            G.did(nc.gpsimd.tensor_copy(tri_le16[:, :], tri_le[:, :]))
            mk["const"] = G.did(nc.gpsimd.tensor_copy(tri_gt16[:, :], tri_gt[:, :]))

            for k in range(KD):
                V.wait(mk["W_inT", k])
                V.did(nc.vector.tensor_reduce(sums[:, k:k + 1], Wstage[:, k, :], AX.X, ALU.max,
                                              apply_absolute_value=True))
            V.wait(V.now())
            r = absmax_scale(sums[:, 0:KD], W_TOP, IN_INV, 0)
            for k in range(KD):
                split(Win[:, 0, k, :], Win[:, 1, k, :], Wstage[:, k, :], tmp[0], r)
            mk["Win"] = [A.now(), V.now()]
            mk["phase"] = [A.now(), V.now()]
            V.wait(mk["W_outT"])
            V.did(nc.vector.tensor_scalar(cw[:, :, :], cw[:, :, :], 0.5, None, ALU.mult))
            mk["cb"] = V.did(nc.vector.tensor_scalar(cb[:, :], cb[:, :], 0.5, None, ALU.mult))
            V.wait(mk["cb"])
            A.wait(mk["W_outT"])
            m = A.did(nc.scalar.activation(negA[:, :], negA[:, :], ACT.Exp))
            V.wait(m)
            mk["negA"] = V.did(nc.vector.tensor_scalar(negA[:, :], negA[:, :], -1.0, None, ALU.mult))

        x1T32 = x1T[:, :, :, :].rearrange("p a k t -> p (a k t)").bitcast(F32).rearrange("p (x d) -> p x d", d=D)
        stageO = [x1[:, :, :], x1T32]
        XH = XT // 2

        def out_weights():
            V.wait(mk["W_outT"])
            for x in range(XT):
                row = stageO[x // XH][:, x % XH, :]
                m = V.did(nc.vector.tensor_scalar(row, row, nw[:, x:x + 1], None, ALU.mult))
            yield
            V.wait(m)
            for i in range(2):
                m = V.did(nc.vector.tensor_reduce(tmp[4 + i], stageO[i], AX.XY, ALU.max, apply_absolute_value=True))
            V.wait(m)
            r = absmax_scale(wsc[:, 14:16], W_TOP * NORM_GAIN, OUT_INV, 2)
            V.wait(r)
            r = V.did(nc.vector.tensor_scalar(tmp[2], tmp[2], 1.0 / NORM_GAIN, None, ALU.mult))
            yield
            for a in range(0, XT, 2):
                src = stageO[a // XH][:, a % XH:a % XH + 2, :].rearrange("p x d -> p (x d)")
                hi, lo = (Wout[:, i, a:a + 2, :].rearrange("p x d -> p (x d)") for i in range(2))
                m = split(hi, lo, src, tmp[2], r)
                yield
            mk["Wout"] = list(m)

        def ffn_weights():
            stage = hid[:, :, :, :].rearrange("p a e t -> p (a e t)").bitcast(F32).rearrange("p (s n) -> p s n", s=2)
            mats = [(W_upT, Wup[:, :, :].rearrange("p k n -> p (k n)"), KD),
                    (W_gateT, Wgate[:, :, :].rearrange("p k n -> p (k n)"), KD),
                    (W_downT, Wdown[:, :, :].rearrange("p k n -> p (k n)"), ET)]
            width = stage.shape[2]
            pieces = DE * D // P // width
            every = [(mat, piece) for mat in range(3) for piece in range(pieces)]

            def load(mat, piece):
                s = next(stage_turn)
                LW[s].wait(stage_read[s])
                src, _, k = mats[mat]
                per = k // pieces
                v = src.rearrange("(x k p) n -> x p k n", p=P, k=per)[piece]
                dst = stage[:, s, :].rearrange("p (k n) -> p k n", k=per)
                return s, LW[s].did(nc.sync.dma_start(dst, v))

            for n, (mat, piece) in enumerate(every):
                s, m = load(mat, piece)
                A.wait(m)
                stage_read[s] = A.did(nc.scalar.activation(stage[:, s, :], stage[:, s, :], ACT.Abs,
                                                           accum_out=sums[:, n:n + 1]))
                yield
            V.wait(A.now())
            m = V.did(nc.vector.tensor_reduce(sum3, sums.rearrange("p (m n) -> p m n", m=3), AX.X, ALU.add))
            G.wait(m)
            m = G.did(nc.gpsimd.partition_all_reduce(tot3, sum3, P, RED.add))
            yield
            V.wait(m)
            m = V.did(nc.vector.tensor_scalar(tot3, tot3, 1.0 / (DE * D), QUANT_EPS, ALU.mult, ALU.add))
            V.wait(m)
            V.did(nc.vector.tensor_scalar(wsc[:, 4:7], tot3, 0.5, None, ALU.mult))
            V.did(nc.vector.tensor_scalar(wsc[:, 7:10], tot3, -0.5, None, ALU.mult))
            V.did(nc.vector.tensor_scalar(UP_T, tot3[:, 0:1], 0.5 / NORM_GAIN, None, ALU.mult))
            m = V.did(nc.vector.tensor_scalar(tmp[7], tot3[:, 0:1], tot3[:, 1:2], 1.0 / HID_GAIN, ALU.mult, ALU.mult))
            V.wait(m)
            scales = V.did(nc.vector.tensor_scalar(FS, tmp[7], tot3[:, 2:3], None, ALU.mult))
            V.wait(scales)
            before = None
            for n, (mat, piece) in enumerate(every):
                s, m = load(mat, piece)
                dst = mats[mat][1][:, piece * width:(piece + 1) * width]
                V.wait(m)
                m = V.did(nc.vector.tensor_scalar(dst, stage[:, s, :], nthr[mat], None, ALU.is_lt, saturate=False))
                if before:
                    finish_sign(*before)
                before = (dst, stage[:, s, :], s, thr[mat], m)
                yield
            finish_sign(*before)
            mk["ffnW"] = V.now()

        def finish_sign(dst, src, s, above, below):
            V.wait(below)
            stage_read[s] = V.did(nc.vector.scalar_tensor_tensor(dst, src, above, dst, ALU.is_gt, ALU.subtract,
                                                                 saturate=False))

        def other_weights():
            out = out_weights()
            for _ in ffn_weights():
                next(out, None)
                yield

        def tile_scalars(par):
            q = sc[:, par, :]
            return [q[:, i:i + 1] for i in range(5)] + [q[:, 5:5 + CT]]

        def scale_u(par):
            umax, uall, su, comb, half, w_last = tile_scalars(par)
            V.wait(mk["uT"])
            m = V.did(nc.vector.tensor_reduce(umax, uTf[:, :, :], AX.XY, ALU.max, apply_absolute_value=True))
            G.wait(m)
            m = G.did(nc.gpsimd.partition_all_reduce(uall, umax, P, RED.max))
            yield
            V.wait(m)
            m = V.did(nc.vector.tensor_scalar(uall, uall, TINY, None, ALU.max))
            V.wait(m)
            m = V.did(nc.vector.reciprocal(su, uall))
            n = V.did(nc.vector.tensor_scalar(comb, uall, IN_INV, 1.0 / U_TOP, ALU.mult, ALU.mult))
            V.wait(m, n)
            mk["su"] = V.did(nc.vector.tensor_scalar(su, su, U_TOP, None, ALU.mult))
            V.did(nc.vector.tensor_scalar(half, comb, 0.5, None, ALU.mult))
            mk["comb", par] = V.did(nc.vector.tensor_scalar(w_last, cw[:, :, HALO], comb, None, ALU.mult))
            yield

        def split_u(par):
            su = tile_scalars(par)[2]
            parts = []
            for k in range(0, KD, 2):
                hi, lo = (uTs[:, i, k:k + 2, :].rearrange("p k t -> p (k t)") for i in range(2))
                A.wait(mk.get("uTs_read"))
                parts += split(hi, lo, uTf[:, k:k + 2, :].rearrange("p k t -> p (k t)"), su, mk["su"])
            mk["uTs"] = parts

        def project(bank, cols, tok, n, width, channels_out):
            for k in range(KD):
                for wi, ui in ((0, 0), (0, 1), (1, 0)):
                    w = Win[:, wi, k, cols:cols + width]
                    x = uTs[:, ui, k, tok:tok + n]
                    i = nc.tensor.matmul(bank, w if channels_out else x, x if channels_out else w,
                                         start=(k == 0 and wi == ui), stop=(k == KD - 1 and wi == 1))
            return PE.did(i)

        def mixer_in(par, fresh):
            pre_turn, acc_turn, tnh_turn = cycle(range(2)), cycle(range(4)), cycle(range(2))
            umax, uall, su, comb, half, w_last = tile_scalars(par)
            if fresh:
                G.wait(mk.get("S_read"), mk.get("S_done"), *(mk.get(("halo", ct)) for ct in range(CT)))
                m = mk["halo_clear"] = G.did(nc.gpsimd.memset(halo[:, :, :], 0.0))
                mk["S_done"] = G.did(nc.gpsimd.memset(S[:, :], 0.0))
                G.wait(m, mk["S_done"])

            def project_dt():
                PE.wait(mk["uTs"])
                b = next(psM_turn)
                bank = psM[b]
                PE.wait(psM_read[b])
                for c in range(NC):
                    p = project(bank[:, c * H:(c + 1) * H], DI + CD, c * P, P, H, False)
                d = [dts[:, i, :] for i in range(10)]

                def bc(v):
                    return v.unsqueeze(1).broadcast_to([P, NC, H])

                def by_chunk(v):
                    return v.rearrange("p (c h) -> p c h", c=NC)

                raw, low, e, s2, q2, pl, dt, a, dldt, s_ = d

                def step(ins):
                    V.wait(V.did(ins))
                v = nc.vector
                V.wait(p, mk["negA"], mk.get("dt_read"), mk["comb", par])
                step(v.scalar_tensor_tensor(by_chunk(raw), by_chunk(bank[:, 0:NC * H]), comb, bc(dtb[:, :]),
                                            ALU.mult, ALU.add))
                psM_read[b] = [V.now()]
                step(v.tensor_scalar(low, raw, -1.0, None, ALU.mult))
                step(v.tensor_tensor(low, low, raw, ALU.min))
                A.wait(V.now())
                V.wait(A.did(nc.scalar.activation(e, low, ACT.Exp)))
                step(v.tensor_scalar(s_, e, 2.0, None, ALU.add))
                step(v.reciprocal(s_, s_))
                step(v.tensor_tensor(s_, s_, e, ALU.mult))
                step(v.tensor_tensor(q2, s_, s_, ALU.mult))
                yield
                step(v.tensor_scalar(pl, q2, 1.0 / 15, None, ALU.mult))
                for odd in (13, 11, 9, 7, 5, 3):
                    step(v.scalar_tensor_tensor(pl, pl, 1.0 / odd, q2, ALU.add, ALU.mult))
                step(v.scalar_tensor_tensor(pl, pl, 1.0, s_, ALU.add, ALU.mult))
                step(v.tensor_scalar(pl, pl, 2.0, None, ALU.mult))
                step(v.scalar_tensor_tensor(dt, raw, 0.0, pl, ALU.max, ALU.add))
                step(v.tensor_tensor(by_chunk(a), by_chunk(dt), bc(negA[:, :]), ALU.mult))
                step(v.tensor_scalar(low, a, A_GAIN, A_FLOOR, ALU.mult, ALU.max))
                V.wait(mk.get("a16_read"))
                step(v.tensor_copy(a16[:, 0, :], low))
                step(v.tensor_tensor(a16[:, 1, :], low, a16[:, 0, :], ALU.subtract))
                mk["a16"] = V.now()

            def decays():
                a, dldt, dt = dts[:, 7, :], dts[:, 8, :], dts[:, 6, :]
                PE.wait(mk["a16"], mk["const"])
                b = next(psM_turn)
                bank = psM[b]
                PE.wait(psM_read[b])
                for i, w in enumerate((tri_le, tri_gt, ones)):
                    p = PE.did(nc.tensor.matmul(bank[:, i * NC * H:(i + 1) * NC * H], w[:, :], a,
                                                start=True, stop=True))
                A.wait(p, mk.get("dec_read"))
                m = A.did(nc.scalar.activation(dec[:, :, :].rearrange("p s n -> p (s n)"), bank[:, 0:3 * NC * H],
                                               ACT.Exp))
                psM_read[b] = [m]
                V.wait(m)
                mk["dec"] = [m, V.did(nc.vector.tensor_tensor(dldt, dec[:, 1, :], dt, ALU.mult))]

            dt_steps = project_dt()
            order = [XT, XT + 1] + list(range(XT))
            live = {}
            LAST = len(order) + 3
            for n in range(LAST):
                if n < len(order):
                    ct = order[n]
                    PE.wait(mk["uTs"], mk["Win"])
                    b = next(psM_turn)
                    bank = psM[b]
                    PE.wait(psM_read[b])
                    p = project(bank[:, :], DI + ct * P, 0, T, P, True)
                    s = next(pre_turn)
                    A.wait(pre_read[s])
                    A.wait(p, mk["comb", par])
                    m1 = A.did(nc.scalar.activation(pre[:, s, 1 + HALO:1 + HALO + T], bank[:, :], ACT.Copy, scale=comb))
                    r = next(acc_turn)
                    A.wait(acc_read[r])
                    A.wait(mk["cb"])
                    m2 = A.did(nc.scalar.activation(acc[:, r, :], bank[:, :], ACT.Identity,
                                                    scale=w_last[:, ct:ct + 1], bias=cb[:, ct:ct + 1]))
                    psM_read[b] = [m1, m2]
                    live[n] = dict(s=s, r=r, m=[m1, m2])
                if 0 <= n - 1 < len(order):
                    ct, w = order[n - 1], live[n - 1]
                    V.wait(pre_read[w["s"]], mk.get(("halo", ct)), mk.get("halo_clear"))
                    m = V.did(nc.vector.tensor_copy(pre[:, w["s"], 1:1 + HALO], halo[:, ct, :]))
                    V.wait(m, w["m"])
                    mk["halo", ct] = V.did(nc.vector.tensor_copy(halo[:, ct, :], pre[:, w["s"], 1 + T:1 + T + HALO]))
                    for tap in range(HALO - 1, -1, -1):
                        m = V.did(nc.vector.scalar_tensor_tensor(acc[:, w["r"], :], pre[:, w["s"], 1 + tap:1 + tap + T],
                                                                 cw[:, ct, tap:tap + 1], acc[:, w["r"], :],
                                                                 ALU.mult, ALU.add))
                        V.wait(m)
                    pre_read[w["s"]] = [m, mk["halo", ct]]
                    w["t"] = next(tnh_turn)
                    A.wait(tnh_read[w["t"]])
                    A.wait(m)
                    w["tanh"] = A.did(nc.scalar.activation(tnh[:, w["t"], :], acc[:, w["r"], :], ACT.Tanh))
                if 0 <= n - 2 < len(order):
                    ct, w = order[n - 2], live[n - 2]
                    if ct == XT:
                        dst = BT[:, :]
                        V.wait(mk.get("BT_read"))
                    elif ct == XT + 1:
                        dst = CTt[:, :]
                        V.wait(mk.get("CT_read"))
                    else:
                        dst = acc[:, w["r"], :]
                    V.wait(w["tanh"])
                    m = V.did(nc.vector.scalar_tensor_tensor(dst, tnh[:, w["t"], :], 1.0, acc[:, w["r"], :],
                                                             ALU.add, ALU.mult))
                    tnh_read[w["t"]] = [m]
                    acc_read[w["r"]] = [m]
                    w["silu"] = m
                    if ct >= XT:
                        mk["BT" if ct == XT else "CT"] = m
                if 0 <= n - 3 < len(order):
                    ct, w = order[n - 3], live[n - 3]
                    if ct != XT + 1:
                        PE.wait(w["silu"], mk["const"])
                        src = BT[:, :] if ct == XT else acc[:, w["r"], :]
                        b = next(psM_turn)
                        bank = psM[b]
                        PE.wait(psM_read[b])
                        for c in range(NC):
                            i = nc.tensor.transpose(bank[:, c * P:(c + 1) * P], src[:, c * P:(c + 1) * P], ident[:, :])
                        p = PE.did(i)
                        if ct != XT:
                            acc_read[w["r"]] = mk["acc_turned"] = p
                        dst = Btok[:, :, :] if ct == XT else xtok[:, :, ct * P:(ct + 1) * P]
                        A.wait(p, mk.get("Btok_read") if ct == XT else mk.get("xtok_read"))
                        m = A.did(nc.scalar.activation(dst, bank[:, :].rearrange("p (c n) -> p c n", c=NC), ACT.Copy))
                        psM_read[b] = [m]
                        mk["Btok" if ct == XT else "xtok"] = m
                if n in (6, 7):
                    next(dt_steps, None)
                if n == 9:
                    decays()
                yield

        def hand_over(*marks):
            for ln in (V, A, G):
                ln.wait(*marks)

        def heads(v, n):
            return v.rearrange("p (h d) -> p h d", h=n)

        HG = DI // P
        HW = T // HD
        halves = [slice(w * T, (w + 1) * T) for w in range(DI // T)]

        def cb_product(c):
            tok = slice(c * P, (c + 1) * P)
            b = next(psM_turn)
            PE.wait(psM_read[b], mk["BT"], mk["CT"])
            p = PE.did(nc.tensor.matmul(psM[b][:, 0:P], BT[:, tok], CTt[:, tok], start=True, stop=True))
            mk["BT_read"] = p
            V.wait(p, mk["const"])
            mk["CBm"] = V.did(nc.vector.tensor_tensor(CBm[:, :], psM[b][:, 0:P], tri_le[:, :], ALU.mult))
            psM_read[b] = mk["CBm"]

        def mask_a(c, g):
            s = next(am_turn)
            G.wait(am_read[s], mk["a16"])
            for part in range(2):
                av = a16[:, part, c * H + g * HG:c * H + (g + 1) * HG]
                m = G.did(nc.gpsimd.tensor_tensor(am[:, 2 * s + part, :].rearrange("p (h i) -> p h i", h=HG),
                                                  av.unsqueeze(2).broadcast_to([P, HG, P]),
                                                  tri_le16[:, :].unsqueeze(1).broadcast_to([P, HG, P]), ALU.mult))
            mk["am", g] = (s, m)
            mk["a16_read"] = m

        def scale_x(c):
            ch = slice(c * H, (c + 1) * H)
            V.wait(mk["xtok"], mk["dec"], mk.get("xdt_read"))
            mk["xdt"] = V.did(nc.vector.tensor_tensor(heads(xdt, H), heads(xtok[:, c, :], H),
                                                      dts[:, 6, ch].unsqueeze(2).broadcast_to([P, H, HD]), ALU.mult))
            mk["xtok_read"] = mk["dt_read"] = [mk["xdt"], mk["yd"]]

        def scale_x_state(c):
            ch = slice(c * H, (c + 1) * H)
            G.wait(mk["xtok"], mk["dec"], mk.get("xs_read"), mk.get("yd_read"))
            mk["xs"] = G.did(nc.gpsimd.tensor_tensor(heads(xs, H), heads(xtok[:, c, :], H),
                                                     dts[:, 8, ch].unsqueeze(2).broadcast_to([P, H, HD]), ALU.mult))
            mk["yd"] = G.did(nc.gpsimd.tensor_tensor(heads(yd, H), heads(xtok[:, c, :], H),
                                                     dskip[:, :].unsqueeze(2).broadcast_to([P, H, HD]), ALU.mult))

        def gate(c, par, w):
            half = sc[:, par, 4:5]
            zw = zs2[:, c % 2, halves[w]]
            b = next(psM_turn)
            PE.wait(psM_read[b], mk["uTs"])
            p = project(psM[b][:, :], w * T, c * P, P, T, False)
            mk["uTs_read"] = p
            A.wait(p, mk.get(("zs_read", c % 2)))
            m = A.did(nc.scalar.activation(zw, psM[b][:, :], ACT.Tanh, scale=half))
            V.wait(m)
            mk["zs", w] = V.did(nc.vector.scalar_tensor_tensor(zw, zw, 1.0, psM[b][:, :], ALU.add, ALU.mult))
            psM_read[b] = mk["zs", w]

        def decay(c):
            for r in range(H // HQ):
                s, m = mk["am", r * HQ // HG]
                b = next(psF_turn)
                PE.wait(psF_read[b], m, mk["const"])
                lo = (r * HQ % HG) * P
                for part in range(2):
                    ins = nc.tensor.matmul(psF[b][:, :], tri_gt16[:, :], am[:, 2 * s + part, lo:lo + T],
                                           start=part == 0, stop=part == 1)
                p = PE.did(ins)
                am_read[s] = p
                Lq = Lm[:, r * HQ:(r + 1) * HQ, :]
                A.wait(p, mk.get("L_read"))
                e = A.did(nc.scalar.activation(Lq, psF[b][:, :].rearrange("p (h i) -> p h i", h=HQ), ACT.Exp,
                                               scale=1.0 / A_GAIN))
                psF_read[b] = e
                V.wait(e, mk["CBm"])
                mk["L", r] = V.did(nc.vector.tensor_tensor(Lq, Lq, CBm[:, :].unsqueeze(1).broadcast_to([P, HQ, P]),
                                                           ALU.mult))

        def y_state(c):
            for w, cols in enumerate(halves):
                b = next(psM_turn)
                PE.wait(psM_read[b], mk["S_done"], mk["CT"])
                p = PE.did(nc.tensor.matmul(psM[b][:, :], CTt[:, c * P:(c + 1) * P], S[:, cols],
                                            start=True, stop=True))
                mk["S_read"] = mk["CT_read"] = p
                grow = dec[:, 0, c * H + w * HW:c * H + (w + 1) * HW]
                V.wait(p, mk.get("y_read"))
                m = V.did(nc.vector.tensor_tensor(heads(y[:, cols], HW), heads(psM[b][:, :], HW),
                                                  grow.unsqueeze(2).broadcast_to([P, HW, HD]), ALU.mult))
                psM_read[b] = m
                mk["y_off", w] = mk["dec_read"] = m

        def new_state(c):
            G.wait(mk["S_read"], mk["S_done"], mk["dec"])
            sd = G.did(nc.gpsimd.tensor_tensor(heads(S[:, :], H), heads(S[:, :], H),
                                               dec[:, 2, c * H:(c + 1) * H].unsqueeze(2).broadcast_to([P, H, HD]),
                                               ALU.mult))
            for cols in halves:
                b = next(psM_turn)
                PE.wait(psM_read[b], mk["xs"], mk["Btok"])
                p = PE.did(nc.tensor.matmul(psM[b][:, :], Btok[:, c, :], xs[:, cols], start=True, stop=True))
                mk["xs_read"] = mk["Btok_read"] = p
                V.wait(p, sd)
                mk["S_done"] = V.did(nc.vector.tensor_tensor(S[:, cols], S[:, cols], psM[b][:, :], ALU.add))
                psM_read[b] = mk["S_done"]
            mk["dec_read"] = [mk["dec_read"], sd]

        def add_skip():
            for w, cols in enumerate(halves):
                G.wait(mk["y_off", w], mk["yd"])
                mk["y_sum", w] = mk["yd_read"] = G.did(nc.gpsimd.tensor_tensor(y[:, cols], y[:, cols], yd[:, cols],
                                                                               ALU.add))

        def y_chunk(c, par, w):
            half, cols = sc[:, par, 4:5], halves[w]
            b = next(psM_turn)
            PE.wait(psM_read[b], mk["xdt"])
            for h in range(w * HW, (w + 1) * HW):
                PE.wait(mk["L", h // HQ])
                ins = nc.tensor.matmul(psM[b][:, (h - w * HW) * HD:(h - w * HW + 1) * HD], Lm[:, h, :],
                                       xdt[:, h * HD:(h + 1) * HD], start=True, stop=True)
            p = PE.did(ins)
            mk["L_read"] = mk["xdt_read"] = p
            V.wait(p, mk["y_sum", w])
            m = V.did(nc.vector.tensor_tensor(y[:, cols], y[:, cols], psM[b][:, :], ALU.add))
            psM_read[b] = m
            V.wait(m, mk["zs", w])
            mk["y"] = V.did(nc.vector.scalar_tensor_tensor(y[:, cols], y[:, cols], half, zs2[:, c % 2, cols],
                                                           ALU.mult, ALU.mult))
            mk["zs_read", c % 2] = mk["y"]

        def rms(c, par):
            ss, r = st[:, par, c, 0:1], st[:, par, c, 1:2]
            A.wait(mk["y"], mk.get("yT_read"))
            squares = yT[:, 0:XT, :].rearrange("p x n -> p (x n)")
            m = A.did(nc.scalar.activation(squares, y, ACT.Square, accum_out=ss))
            G.wait(m)
            m = G.did(nc.gpsimd.tensor_scalar(r, ss, 1.0 / DI, RMS_EPS, ALU.mult, ALU.add))
            G.wait(m)
            m = G.did(nc.gpsimd.tensor_tensor(r, r, minus_half[:, :], ALU.pow))
            A.wait(m)
            mk["yn"] = A.did(nc.scalar.activation(y, y, ACT.Copy, scale=r))

        def row_stats(c, par, col, h):
            s6, mv, r, nm = (st[:, par, c, a:b] for a, b in ((col, col + 6), (14, 16), (12, 13), (13, 14)))
            V.wait(h)
            m = V.did(nc.vector.bn_stats(s6, x1[:, c, :]))
            V.wait(m)
            m = V.did(nc.vector.bn_aggr(mv, s6))
            G.wait(m)
            m = G.did(nc.gpsimd.tensor_scalar(r, mv[:, 1:2], LN_EPS, None, ALU.add))
            G.wait(m)
            m = G.did(nc.gpsimd.tensor_tensor(r, r, minus_half[:, :], ALU.pow))
            G.wait(m)
            return G.did(nc.gpsimd.tensor_scalar(nm, mv[:, 0:1], r, -1.0, ALU.mult, ALU.mult))

        def normalise(c, par, stats):
            r, nm = st[:, par, c, 12:13], st[:, par, c, 13:14]
            A.wait(stats)
            return A.did(nc.scalar.activation(x1[:, c, :], x1[:, c, :], ACT.Identity, bias=nm, scale=r))

        def turn_y(c):
            XB = T // P
            for w in range(XT // XB):
                b = next(psM_turn)
                PE.wait(psM_read[b], mk["yn"])
                for x in range(XB):
                    ins = nc.tensor.transpose(psM[b][:, x * P:(x + 1) * P], y[:, (XB * w + x) * P:(XB * w + x + 1) * P],
                                              ident[:, :])
                p = PE.did(ins)
                mk["y_read"] = p
                hi, lo = (yT[:, i * XT + XB * w:i * XT + XB * w + XB, :].rearrange("p x n -> p (x n)")
                          for i in range(2))
                A.wait(p, mk.get("yT_read"))
                m = A.did(nc.scalar.activation(hi, psM[b][:, :], ACT.Copy, scale=NORM_GAIN))
                V.wait(m)
                mk["yT", w] = V.did(nc.vector.scalar_tensor_tensor(lo, psM[b][:, :], NORM_GAIN, hi,
                                                                   ALU.mult, ALU.subtract))
                psM_read[b] = mk["yT", w]

        def load_res(t, c):
            LR[c % 2].wait(mk.get(("res_read", c % 2)))
            mk["res", c] = LR[c % 2].did(nc.sync.dma_start(res[:, c % 2, :], u_v[:, t, c, :]))

        def project_out(c, par):
            b = next(psM_turn)
            PE.wait(psM_read[b], mk["Wout"])
            for x in range(XT):
                PE.wait(mk["yT", x // (T // P)])
                for yi, wi in ((0, 0), (0, 1), (1, 0)):
                    ins = nc.tensor.matmul(psM[b][:, :], yT[:, yi * XT + x, :], Wout[:, wi, x, :],
                                           start=(x == 0 and yi == wi), stop=(x == XT - 1 and yi == 1))
            p = PE.did(ins)
            mk["yT_read"] = p
            V.wait(p, mk["res", c], mk.get(("stored", c)))
            h = V.did(nc.vector.scalar_tensor_tensor(x1[:, c, :], psM[b][:, :], OUT_INV, res[:, c % 2, :],
                                                     ALU.mult, ALU.add))
            psM_read[b] = h
            mk["res_read", c % 2] = h
            mk["x1_stats", c] = row_stats(c, par, 2, h)

        def turn_x1(c):
            b = next(psM_turn)
            PE.wait(psM_read[b], mk["x1", c])
            for k in range(KD):
                ins = nc.tensor.transpose(psM[b][:, k * P:(k + 1) * P], x1[:, c, k * P:(k + 1) * P], ident[:, :])
            p = PE.did(ins)
            hi, lo = (x1T[:, i, :, c * P:(c + 1) * P] for i in range(2))
            bv = psM[b][:, :].rearrange("p (k n) -> p k n", k=KD)
            A.wait(p, mk.get("x1T_read"))
            m = A.did(nc.scalar.activation(hi, bv, ACT.Copy, scale=NORM_GAIN))
            V.wait(m)
            l = V.did(nc.vector.scalar_tensor_tensor(lo, bv, NORM_GAIN, hi, ALU.mult, ALU.subtract))
            psM_read[b] = l
            mk["x1T_new", c] = l

        def ffn_up(half):
            live = {}
            for n in range(EH + 1):
                if n < EH:
                    e = half * EH + n
                    PE.wait(mk["x1T"], mk.get("ffnW"))
                    ps = []
                    for Wm in (Wup, Wgate):
                        b = next(psF_turn)
                        bank = psF[b]
                        PE.wait(psF_read[b])
                        for k in range(KD):
                            for i in range(2):
                                ins = nc.tensor.matmul(bank[:, :], Wm[:, k, e * P:(e + 1) * P], x1T[:, i, k, :],
                                                       start=(k == 0 and i == 0), stop=(k == KD - 1 and i == 1))
                        ps.append((bank, b, PE.did(ins)))
                    mk["x1T_read"] = ps[1][2]
                    (Ub, ub, up), (Gb, gb, gp) = ps
                    t = next(fth_turn)
                    A.wait(fth_read[t])
                    A.wait(up)
                    m = A.did(nc.scalar.activation(fth[:, t, :], Ub[:, :], ACT.Tanh, scale=UP_T))
                    live[n] = (t, m, Ub, ub, Gb, gb, gp)
                if n >= 1:
                    t, m, Ub, ub, Gb, gb, gp = live[n - 1]
                    q = next(fp_turn)
                    V.wait(fp_read[q])
                    V.wait(m)
                    m = V.did(nc.vector.scalar_tensor_tensor(fp[:, q, :], fth[:, t, :], 1.0, Ub[:, :],
                                                             ALU.add, ALU.mult))
                    fth_read[t] = [m]
                    psF_read[ub] = [m]
                    f = next(fh_turn)
                    V.wait(fh_read[f])
                    V.wait(m, gp)
                    m = V.did(nc.vector.scalar_tensor_tensor(fh[:, f, :], fp[:, q, :],
                                                             0.5 * HID_GAIN / NORM_GAIN ** 2, Gb[:, :],
                                                             ALU.mult, ALU.mult))
                    fp_read[q] = [m]
                    psF_read[gb] = [m]
                    A.wait(m, mk.get("hid_read"))
                    h = A.did(nc.scalar.activation(hid[:, 0, n - 1, :], fh[:, f, :], ACT.Copy))
                    V.wait(h, m, mk.get("hid_read"))
                    l = V.did(nc.vector.tensor_tensor(hid[:, 1, n - 1, :], fh[:, f, :], hid[:, 0, n - 1, :],
                                                      ALU.subtract))
                    fh_read[f] = [h, l]
                    mk["hid", n - 1] = [h, l]
                yield

        def ffn_down(half, c):
            b = next(psF_turn)
            bank = psF[b]
            PE.wait(psF_read[b])
            for n in range(EH):
                PE.wait(mk["hid", n])
                for i in range(2):
                    ins = nc.tensor.matmul(bank[:, :], hid[:, i, n, c * P:(c + 1) * P], Wdown[:, half * EH + n, :],
                                           start=(n == 0 and i == 0), stop=(n == EH - 1 and i == 1))
            p = PE.did(ins)
            mk["hid_read"] = p
            V.wait(p, mk["x1", c])
            m = V.did(nc.vector.scalar_tensor_tensor(x1[:, c, :], bank[:, :], FS, x1[:, c, :], ALU.mult, ALU.add))
            psF_read[b] = [m]
            mk["x1", c] = m

        def ffn_last(c, par):
            ffn_down(1, c)
            mk["out_stats", c] = row_stats(c, 1 - par, 2, mk["x1", c])

        def ffn_store(c, par, t):
            n = normalise(c, 1 - par, mk["out_stats", c])
            ST[c].wait(n)
            mk["stored", c] = ST[c].did(nc.sync.dma_start(out_v[:, t, c, :], x1[:, c, :]))

        def ffn_first():
            mk["x1T"] = [mk.get(("x1T_new", c)) for c in range(NC)]
            yield from ffn_up(0)
            for c in range(NC):
                ffn_down(0, c)
                yield
            yield from ffn_up(1)

        def run(gen):
            for _ in gen:
                pass

        def phase2(par, mixer_t, ffn_t, ffn_rest, early, filler=None):
            next_u = scale_u(1 - par)
            ahead = 1 if early else 0
            load_res(mixer_t, 0)
            load_res(mixer_t, 1)
            G.wait(mk["acc_turned"], V.now(), A.now())
            mask_a(0, 0)
            mask_a(0, 1)
            scale_x_state(0)
            cb_product(0)
            next(ffn_rest, None)
            next(ffn_rest, None)
            gate(0, par, 0)
            run(ffn_rest)
            gate(0, par, 1)
            hand_over(mk["acc_turned"], V.now(), A.now())
            scale_x(0)
            decay(0)
            for c in range(NC):
                last = c + 1 == NC
                f = c + ahead
                y_state(c)
                new_state(c)
                add_skip()
                if not last:
                    mask_a(c + 1, 0)
                if c == 0 and ffn_t is not None and ahead:
                    ffn_last(0, par)
                    ffn_store(0, par, ffn_t)
                if c:
                    mk["x1", c - 1] = normalise(c - 1, par, mk["x1_stats", c - 1])
                if early:
                    if last:
                        split_u(1 - par)
                    else:
                        next(next_u, None)
                y_chunk(c, par, 0)
                if c:
                    turn_x1(c - 1)
                y_chunk(c, par, 1)
                rms(c, par)
                if last:
                    hand_over(PE.now(), V.now(), mk["yn"], G.now())
                    for _ in range(2 * ahead):
                        next(early)
                else:
                    cb_product(c + 1)
                    gate(c + 1, par, 0)
                    mask_a(c + 1, 1)
                if ffn_t is not None and f < NC:
                    ffn_last(f, par)
                turn_y(c)
                if filler:
                    for _ in range(3):
                        next(filler, None)
                if ffn_t is not None and f < NC:
                    ffn_store(f, par, ffn_t)
                if not last:
                    gate(c + 1, par, 1)
                    scale_x(c + 1)
                    scale_x_state(c + 1)
                    decay(c + 1)
                elif early:
                    next(early)
                project_out(c, par)
                if c + 2 < NC:
                    load_res(mixer_t, c + 2)
            if early:
                next(early)
            mk["x1", NC - 1] = normalise(NC - 1, par, mk["x1_stats", NC - 1])
            if early:
                next(early)
            turn_x1(NC - 1)

        def tile(par, mixer_t, ffn_t, inputs, early):
            if early:
                load_uT(mixer_t + 1, mk["uTs"])
            ffn = ffn_first()
            next(inputs)
            drain((inputs, MIXER_STEPS - EARLY - 1), (ffn, FFN_STEPS - 4))
            phase2(par, mixer_t, ffn_t, ffn, early)

        MIXER_STEPS = CT + 3
        EARLY = 5
        FFN_STEPS = 2 * (EH + 1) + NC
        setup()
        A.wait(mk["phase"])
        G.wait(mk["phase"])
        run(scale_u(0))
        split_u(0)
        load_uT(1, mk["uTs"])
        weights = other_weights()
        drain((mixer_in(0, True), MIXER_STEPS), (weights, 15))
        odd = mixer_in(1, False)
        phase2(0, 0, None, iter(()), odd, weights)
        run(weights)
        barrier()
        with nc.Fori(0, NT // 2 - 1) as i:
            even, next_odd = mixer_in(0, True), mixer_in(1, False)
            tile(1, 2 * i + 1, 2 * i, odd, even)
            tile(0, 2 * i + 2, 2 * i + 1, even, next_odd)
            barrier()
        tile(1, NT - 1, NT - 2, next_odd, None)
        run(ffn_first())
        for c in range(NC):
            ffn_last(c, 0)
            ffn_store(c, 0, NT - 1)
        for c in range(NC):
            SP.wait(ST[c].now())



_INS = ["u", "uT", "W_inT", "conv_w", "conv_b", "dt_bias", "A_log", "Dp", "norm_w", "W_outT", "W_upT", "W_gateT",
        "W_downT"]


def kernel(**inputs):
    import numpy as np
    import concourse.bacc as bacc
    from concourse import mybir as _mybir
    from concourse.bass_utils import run_bass_kernel_spmd

    g = {k: np.asarray(v) for k, v in inputs.items()}
    u = g["L0_attn_u"]
    rows = {
        "u": u,
        "uT": u.reshape(-1, u.shape[-1]).T,
        "W_inT": g["L0_attn_W_in"].T,
        "conv_w": g["L0_attn_conv_w"],
        "conv_b": g["L0_attn_conv_b"],
        "dt_bias": g["L0_attn_dt_bias"],
        "A_log": g["L0_attn_A_log"],
        "Dp": g["L0_attn_Dp"],
        "norm_w": g["L0_attn_norm_w"],
        "W_outT": g["L0_attn_W_out"].T,
        "W_upT": g["L0_ffn_W_up"].T,
        "W_gateT": g["L0_ffn_W_gate"].T,
        "W_downT": g["L0_ffn_W_down"].T,
    }
    nc = bacc.Bacc("TRN2", target_bir_lowering=False, num_devices=1)
    arrays, args = {}, []
    for name in _INS:
        a = np.ascontiguousarray(rows[name])
        arrays[f"in_{name}"] = a
        args.append(nc.dram_tensor(f"in_{name}", a.shape, _mybir.dt.from_np(a.dtype), kind="ExternalInput").ap())
    args.append(nc.dram_tensor("out_y", u.shape, _mybir.dt.from_np(u.dtype), kind="ExternalOutput").ap())
    build(nc, *args)
    r = run_bass_kernel_spmd(nc, [arrays], core_ids=[0])
    return r.results[0]["out_y"]
```

```python
from contextlib import ExitStack
from itertools import chain, cycle

import concourse.bass as bass
from concourse import mybir

ALU = mybir.AluOpType
ACT = mybir.ActivationFunctionType
AX = mybir.AxisListType
F32 = mybir.dt.float32
F16 = mybir.dt.float16
F8 = mybir.dt.float8e4
RED = bass.bass_isa.ReduceOp

P = 128
U_TOP = 1024.0
W_TOP = 32768.0
A_GAIN = 256.0
A_FLOOR = -60000.0
NORM_GAIN = 1024.0
HID_GAIN = 1.0 / 8.0
LN_EPS = 1e-5
RMS_EPS = 1e-5
QUANT_EPS = 1e-8
TINY = 1e-30


class Line:

    def __init__(self, clock, eng, sem, step=1):
        self.clock, self.eng, self.sem, self.step = clock, eng, sem, step
        self.count = 0
        self.seen = {}
        clock.lines.append(self)

    def did(self, ins):
        ins.then_inc(self.sem, self.step)
        self.count += self.step
        return (self.clock.epoch, self, self.count)

    def wait(self, *marks):
        for m in marks:
            if m is None:
                continue
            if isinstance(m, list):
                self.wait(*m)
                continue
            epoch, line, value = m
            if epoch == self.clock.epoch and self.seen.get(line.sem, 0) < value:
                self.eng.wait_ge(line.sem, value)
                self.seen[line.sem] = value

    def now(self):
        return (self.clock.epoch, self, self.count) if self.count else None


class Clock:
    def __init__(self):
        self.epoch = 0
        self.lines = []

    def turn(self):
        self.epoch += 1
        for line in self.lines:
            line.count = 0
            line.seen = {}


def drain(*steps):
    total = max(n for _, n in steps)
    done = [0] * len(steps)
    for k in range(1, total + 1):
        for i, (gen, n) in enumerate(steps):
            while done[i] < (k * n + total - 1) // total:
                next(gen, None)
                done[i] += 1


def build(nc, u, uT, W_inT, conv_w, conv_b, dt_bias, A_log, Dp, norm_w, W_outT, W_upT, W_gateT, W_downT, out):
    B, L, D = u.shape
    DI = W_outT.shape[0]
    H = Dp.shape[0]
    CD = conv_w.shape[0]
    NS = (CD - DI) // 2
    HD = DI // H
    DE = W_upT.shape[1]
    DP = W_inT.shape[1]
    TAPS = conv_w.shape[1]
    HALO = TAPS - 1
    T = 512
    NT = B * L // T
    NC = T // P
    KD = D // P
    CT = CD // P
    XT = DI // P
    ET = DE // P
    EH = ET // 2
    ZW = DI // T
    HB = T // HD
    HQ = T // P
    assert L == 2 * T and NS == P and DI % T == 0 and D == T and HD * 2 == P

    clock = Clock()
    with ExitStack() as ctx:
        def sb(name, shape, dt=F32):
            return ctx.enter_context(nc.sbuf_tensor(name, shape, dt))

        ident = sb("ident", [P, P])
        tri_le = sb("tri_le", [P, P])
        tri_gt = sb("tri_gt", [P, P])
        ones = sb("ones", [P, P])
        tri_le16 = sb("tri_le16", [P, P], F16)
        tri_gt16 = sb("tri_gt16", [P, P], F16)
        minus_half = sb("minus_half", [P, 1])
        cw = sb("cw", [P, CT, TAPS])
        cb = sb("cb", [P, CT])
        dtb = sb("dtb", [P, H])
        negA = sb("negA", [P, H])
        dskip = sb("dskip", [P, H])
        nw = sb("nw", [P, XT])
        Win = sb("Win", [P, 2, KD, DP], F16)
        Wout = sb("Wout", [P, 2, XT, D], F16)
        Wup = sb("Wup", [P, KD, DE], F8)
        Wgate = sb("Wgate", [P, KD, DE], F8)
        Wdown = sb("Wdown", [P, ET, D], F8)
        wsc = sb("wsc", [P, 54])
        uTf = sb("uTf", [P, KD, T])
        uTs = sb("uTs", [P, 2, KD, T], F16)
        halo = sb("halo", [P, CT, HALO])
        BT = sb("BT", [P, T])
        CTt = sb("CTt", [P, T])
        Btok = sb("Btok", [P, NC, P])
        xtok = sb("xtok", [P, NC, DI])
        S = sb("S", [P, DI])
        x1 = sb("x1", [P, NC, D])
        x1T = sb("x1T", [P, 2, KD, T], F16)
        hid = sb("hid", [P, 2, EH, T], F16)
        dts = sb("dts", [P, 10, NC * H])
        a16 = sb("a16", [P, 2, NC * H], F16)
        dec = sb("dec", [P, 3, NC * H])
        sc = sb("sc", [P, 2, 16])
        st = sb("st", [P, 2, NC, 16])
        CBm = sb("CBm", [P, P])
        WORK = 11272
        work = sb("work", [P, WORK])
        res = sb("res", [P, 2, D])

        def cut(start, shape, dt=F32):
            n = 1
            for s in shape:
                n *= s
            words = n // (2 if dt == F16 else 1)
            v = work[:, start:start + words]
            if dt != F32:
                v = v.bitcast(dt)
            if len(shape) == 2:
                v = v.rearrange("p (a b) -> p a b", a=shape[0])
            return v, start + words

        at = 0
        pre, at = cut(at, [2, HALO + 1 + T])
        acc, at = cut(at, [4, T])
        tnh, at = cut(at, [2, T])
        mixer_end = at
        fth, at = cut(at, [2, T])
        fp, at = cut(at, [2, T])
        fh, at = cut(at, [2, T])
        phase1_end = at
        at = 0
        am, at = cut(at, [4, DI], F16)
        xs, at = cut(at, [DI])
        yd, at = cut(at, [DI])
        assert at <= mixer_end
        at = mixer_end
        xdt, at = cut(at, [DI])
        Lm, at = cut(at, [H, P])
        at = max(at, phase1_end)
        y, at = cut(at, [DI])
        zs2, at = cut(at, [2, DI])
        yT, at = cut(at, [2 * XT, P], F16)
        assert at <= WORK
        NBC = DP - 2 * DI
        z_stage, at = cut(mixer_end, [KD, DI])
        bc_stage, at = cut(at, [KD, NBC])
        bc_abs, at = cut(at, [KD, NBC])
        assert at <= WORK
        x_stage = hid[:, :, :, :].rearrange("p a e t -> p (a e t)").bitcast(F32).rearrange("p (k n) -> p k n", k=KD)

        psM = [ctx.enter_context(nc.psum_tensor(f"psM{i}", [P, T], F32)) for i in range(4)]
        psF = [ctx.enter_context(nc.psum_tensor(f"psF{i}", [P, T], F32)) for i in range(4)]

        sems = []

        def line(eng, name, step=1):
            s = ctx.enter_context(nc.semaphore(name))
            sems.append(s)
            return Line(clock, eng, s, step)

        PE = line(nc.tensor, "pe_done")
        V = line(nc.vector, "dve_done")
        A = line(nc.scalar, "act_done")
        G = line(nc.gpsimd, "pool_done")
        LU = line(nc.sync, "uT_loaded", 16)
        LR = [line(nc.sync, f"u_loaded{c}", 16) for c in range(NC)]
        ST = [line(nc.sync, f"y_stored{c}", 16) for c in range(NC)]
        LS = line(nc.sync, "small_loaded", 16)
        LB = line(nc.sync, "bc_loaded", 16)
        LX = [line(nc.sync, f"x_loaded{k}", 16) for k in range(KD)]
        LZ = line(nc.sync, "z_loaded", 16)
        LO = [line(nc.sync, f"w_out_loaded{i}", 16) for i in range(2)]
        LW = [line(nc.sync, f"ffn_loaded{i}", 16) for i in range(2)]
        SP = Line(clock, nc.sync, None)

        def barrier():
            for ln in [LU, LS, LB, LZ, *LX, *LO, *LR, *ST, *LW]:
                SP.wait(ln.now())
            nums = sorted(s.num for s in sems)
            assert nums == list(range(nums[0], nums[0] + len(nums)))
            nc.all_engine_barrier(sems_to_clear=range(nums[0], nums[-1] + 1))
            clock.turn()

        psM_turn, psF_turn = cycle(range(4)), cycle(range(4))
        am_turn = cycle(range(2))
        fth_turn, fp_turn, fh_turn, stage_turn = cycle(range(2)), cycle(range(2)), cycle(range(2)), cycle(range(2))
        psM_read, psF_read = [None] * 4, [None] * 4
        pre_read, acc_read, tnh_read, am_read = [None] * 2, [None] * 4, [None] * 2, [None] * 2
        fth_read, fp_read, fh_read, stage_read = [None] * 2, [None] * 2, [None] * 2, [None] * 2

        IN_INV, OUT_INV, UP_T, FS = (wsc[:, i:i + 1] for i in range(4))
        Z_INV = wsc[:, 38:39]
        abs_x, abs_z, abs_out = wsc[:, 40:41 + KD], wsc[:, 41 + KD:41 + 2 * KD], wsc[:, 41 + 2 * KD:45 + 2 * KD]
        tmp = [wsc[:, 10 + i:11 + i] for i in range(8)]
        sums = wsc[:, 20:20 + 12]
        tot3 = wsc[:, 32:35]
        sum3 = wsc[:, 35:38]

        uT_v = uT.rearrange("(k p) (t n) -> p k t n", p=P, n=T)
        u_v = u.rearrange("b (h c p) d -> p (b h) c d", p=P, c=NC)
        out_v = out.rearrange("b (h c p) d -> p (b h) c d", p=P, c=NC)

        mk = {}

        def load_uT(t, *after):
            LU.wait(*after)
            mk["uT"] = LU.did(nc.sync.dma_start(uTf[:, :, :], uT_v[:, :, t, :]))

        def sum_scale(src, top, out_inv, col):
            m = V.did(nc.vector.tensor_reduce(tmp[col], src, AX.X, ALU.max))
            G.wait(m)
            m = G.did(nc.gpsimd.partition_all_reduce(tmp[col + 1], tmp[col], P, RED.max))
            V.wait(m)
            m = V.did(nc.vector.tensor_scalar(tmp[col + 1], tmp[col + 1], TINY, None, ALU.max))
            V.wait(m)
            V.did(nc.vector.tensor_scalar(out_inv, tmp[col + 1], 1.0 / top, None, ALU.mult))
            m = V.did(nc.vector.reciprocal(tmp[col], tmp[col + 1]))
            V.wait(m)
            return V.did(nc.vector.tensor_scalar(tmp[col], tmp[col], top, None, ALU.mult))

        def abs_sum(total, src, junk, *after):
            A.wait(*after)
            return A.did(nc.scalar.activation(junk, src, ACT.Abs, accum_out=total))

        def split(hi, lo, src, scale, after):
            A.wait(after)
            h = A.did(nc.scalar.activation(hi, src, ACT.Copy, scale=scale))
            V.wait(h, after)
            return [h, V.did(nc.vector.scalar_tensor_tensor(lo, src, scale, hi, ALU.mult, ALU.subtract))]

        def split_steps(pieces, after):
            before = None
            for piece in pieces + [None]:
                if piece:
                    name, hi, lo, src, scale = piece
                    A.wait(after)
                    h = A.did(nc.scalar.activation(hi, src, ACT.Copy, scale=scale))
                if before:
                    name_, hi_, lo_, src_, scale_, h_ = before
                    V.wait(h_, after)
                    mk[name_] = [h_, V.did(nc.vector.scalar_tensor_tensor(lo_, src_, scale_, hi_, ALU.mult,
                                                                          ALU.subtract))]
                before = piece and (name, hi, lo, src, scale, h)
                yield

        def setup():
            W_in_v = W_inT.rearrange("(k p) n -> p k n", p=P)
            load_uT(0)
            mk["bc_in"] = LB.did(nc.sync.dma_start(bc_stage, W_in_v[:, :, 2 * DI:]))
            for k in range(KD):
                mk["x_in", k] = LX[k].did(nc.sync.dma_start(x_stage[:, k, :], W_in_v[:, k, DI:2 * DI]))
            small = [
                (cw[:, :, :], conv_w.rearrange("(c p) w -> p c w", p=P)),
                (cb[:, :], conv_b.rearrange("(c p) -> p c", p=P)),
                (dtb[:, :], dt_bias.partition_broadcast(P)),
                (negA[:, :], A_log.partition_broadcast(P)),
                (dskip[:, :], Dp.partition_broadcast(P)),
                (nw[:, :], norm_w.rearrange("(c p) -> p c", p=P)),
            ]
            with nc.allow_non_contiguous_dma("small parameters"):
                for dst, src in small:
                    mk["small"] = LS.did(nc.sync.dma_start(dst, src))
            for i in range(2):
                mk["W_outT", i] = LO[i].did(nc.sync.dma_start(stageO[i], W_outT.rearrange("(i x p) d -> i p x d", p=P,
                                                                                         x=XH)[i]))
            mk["z_in"] = LZ.did(nc.sync.dma_start(z_stage, W_in_v[:, :, 0:DI]))

            m = G.did(nc.gpsimd.memset(ones[:, :], 1.0))
            G.did(nc.gpsimd.memset(minus_half[:, :], -0.5))
            G.wait(m)
            G.did(nc.gpsimd.affine_select(out=ident[:, :], in_=ones[:, :], compare_op=ALU.is_equal, fill=0.0,
                                          base=0, pattern=[[-1, P]], channel_multiplier=1))
            G.did(nc.gpsimd.affine_select(out=tri_le[:, :], in_=ones[:, :], compare_op=ALU.is_ge, fill=0.0,
                                          base=0, pattern=[[1, P]], channel_multiplier=-1))
            m = G.did(nc.gpsimd.affine_select(out=tri_gt[:, :], in_=ones[:, :], compare_op=ALU.is_gt, fill=0.0,
                                              base=0, pattern=[[-1, P]], channel_multiplier=1))
            G.wait(m)
            G.did(nc.gpsimd.tensor_copy(tri_le16[:, :], tri_le[:, :]))
            mk["const"] = G.did(nc.gpsimd.tensor_copy(tri_gt16[:, :], tri_gt[:, :]))

            u_scale = scale_u(0)
            next(u_scale)
            m = [abs_sum(abs_x[:, KD:KD + 1], bc_stage.rearrange("p k n -> p (k n)"),
                         bc_abs.rearrange("p k n -> p (k n)"), mk["bc_in"])]
            for k in range(KD):
                m.append(abs_sum(abs_x[:, k:k + 1], x_stage[:, k, :], xtok[:, k, :], mk["x_in", k]))
            mk["xtok_read"] = m
            next(u_scale)
            split_u(0)
            V.wait(m)
            mk["x_scale"] = sum_scale(abs_x, W_TOP, IN_INV, 0)
            V.wait(mk["x_scale"], mk["small"])
            V.did(nc.vector.tensor_scalar(cw[:, :, :], cw[:, :, :], 0.5, None, ALU.mult))
            mk["cb"] = V.did(nc.vector.tensor_scalar(cb[:, :], cb[:, :], 0.5, None, ALU.mult))
            V.wait(mk["cb"])
            next(u_scale)
            load_uT(1, mk["uTs"])
            A.wait(mk["small"])
            m = A.did(nc.scalar.activation(negA[:, :], negA[:, :], ACT.Exp))
            V.wait(m)
            mk["negA"] = V.did(nc.vector.tensor_scalar(negA[:, :], negA[:, :], -1.0, None, ALU.mult))
            for x in range(XT):
                row = stageO[x // XH][:, x % XH, :]
                G.wait(mk["small"], mk["W_outT", x // XH])
                mk["W_out_scaled", x // XH] = G.did(nc.gpsimd.tensor_tensor(row, row, nw[:, x:x + 1].broadcast_to([P, D]),
                                                                           ALU.mult))

        def in_weights():
            def part(name, col, src, scale):
                n = src.shape[2]
                return ("Win", name), Win[:, 0, :, col:col + n], Win[:, 1, :, col:col + n], src, scale

            yield from split_steps(
                [part(XT, 2 * DI, bc_stage[:, :, 0:P], tmp[0]),
                 part(XT + 1, 2 * DI + P, bc_stage[:, :, P:2 * P], tmp[0])] +
                [part(x, DI + x * P, x_stage[:, :, x * P:(x + 1) * P], tmp[0]) for x in range(XT // 2)] +
                [part("dt", 2 * DI + 2 * P, bc_stage[:, :, 2 * P:], tmp[0])] +
                [part(x, DI + x * P, x_stage[:, :, x * P:(x + 1) * P], tmp[0]) for x in range(XT // 2, XT)],
                mk["x_scale"])
            mk["zs_read", 0] = mk["zs_read", 1] = mk["Win", "dt"]
            stage_read[0] = stage_read[1] = mk["Win", XT - 1]
            m = None
            for k in range(KD):
                m = abs_sum(abs_z[:, k:k + 1], z_stage[:, k, :], junk, mk["z_in"], m)
                if k % 2:
                    yield
            yield
            V.wait(m)
            r = sum_scale(abs_z, W_TOP, Z_INV, 4)
            yield from split_steps([part("z", q, z_stage[:, :, q:q + DI // 4], tmp[4])
                                    for q in range(0, DI, DI // 4)], r)
            mk["z_abs"] = m

        junk = Wdown[:, :, :].rearrange("p e d -> p (e d)").bitcast(F32)[:, 0:DI]
        x1T32 = x1T[:, :, :, :].rearrange("p a k t -> p (a k t)").bitcast(F32).rearrange("p (x d) -> p x d", d=D)
        stageO = [x1[:, :, :], x1T32]
        XH = XT // 2

        def out_weights():
            m = mk["z_abs"]
            for a in range(0, XT, 2):
                src = stageO[a // XH][:, a % XH:a % XH + 2, :].rearrange("p x d -> p (x d)")
                m = abs_sum(abs_out[:, a // 2:a // 2 + 1], src, junk, mk["W_out_scaled", a // XH], m)
                if a % 4:
                    yield
            mk["junk"] = m
            yield
            V.wait(m)
            r = sum_scale(abs_out, W_TOP * NORM_GAIN, OUT_INV, 2)
            V.wait(r)
            r = V.did(nc.vector.tensor_scalar(tmp[2], tmp[2], 1.0 / NORM_GAIN, None, ALU.mult))
            pairs = []
            for a in range(0, XT, 2):
                hi, lo = (Wout[:, i, a:a + 2, :].rearrange("p x d -> p (x d)") for i in range(2))
                src = stageO[a // XH][:, a % XH:a % XH + 2, :].rearrange("p x d -> p (x d)")
                pairs.append(("Wout", hi, lo, src, tmp[2]))
            yield from split_steps(pairs, r)

        def ffn_weights():
            stage = hid[:, :, :, :].rearrange("p a e t -> p (a e t)").bitcast(F32).rearrange("p (s n) -> p s n", s=2)
            mats = [(W_upT, Wup[:, :, :].rearrange("p k n -> p (k n)"), KD),
                    (W_gateT, Wgate[:, :, :].rearrange("p k n -> p (k n)"), KD),
                    (W_downT, Wdown[:, :, :].rearrange("p k n -> p (k n)"), ET)]
            width = stage.shape[2]
            pieces = DE * D // P // width
            coming = iter([(mat, piece) for mat in range(3) for _ in range(2) for piece in range(pieces)])

            def load(mat, piece):
                s = next(stage_turn)
                LW[s].wait(stage_read[s])
                src, _, k = mats[mat]
                per = k // pieces
                v = src.rearrange("(x k p) n -> x p k n", p=P, k=per)[piece]
                dst = stage[:, s, :].rearrange("p (k n) -> p k n", k=per)
                return s, LW[s].did(nc.sync.dma_start(dst, v))

            def load_next():
                following = next(coming, None)
                if following:
                    loaded.append(load(*following))

            loaded = []
            load_next()
            load_next()
            for mat in range(3):
                for piece in range(pieces):
                    s, m = loaded.pop(0)
                    A.wait(m)
                    n = mat * pieces + piece
                    stage_read[s] = A.did(nc.scalar.activation(stage[:, s, :], stage[:, s, :], ACT.Abs,
                                                               accum_out=sums[:, n:n + 1]))
                    load_next()
                    yield
                mean, upper, lower = (wsc[:, i + mat:i + mat + 1] for i in (32, 4, 7))
                V.wait(stage_read[s])
                m = V.did(nc.vector.tensor_reduce(sum3[:, mat:mat + 1], sums[:, mat * pieces:(mat + 1) * pieces],
                                                  AX.X, ALU.add))
                G.wait(m)
                m = G.did(nc.gpsimd.partition_all_reduce(mean, sum3[:, mat:mat + 1], P, RED.add))
                yield
                V.wait(m)
                m = V.did(nc.vector.tensor_scalar(mean, mean, 1.0 / (DE * D), QUANT_EPS, ALU.mult, ALU.add))
                V.wait(m)
                V.did(nc.vector.tensor_scalar(upper, mean, 0.5, None, ALU.mult))
                scales = V.did(nc.vector.tensor_scalar(lower, mean, -0.5, None, ALU.mult))
                V.wait(scales)
                for piece in range(pieces):
                    s, m = loaded.pop(0)
                    dst = mats[mat][1][:, piece * width:(piece + 1) * width]
                    V.wait(m, mk["junk"] if mat == 2 else None)
                    m = V.did(nc.vector.tensor_scalar(dst, stage[:, s, :], lower, None, ALU.is_lt, saturate=False))
                    V.wait(m)
                    stage_read[s] = V.did(nc.vector.scalar_tensor_tensor(dst, stage[:, s, :], upper, dst, ALU.is_gt,
                                                                         ALU.subtract, saturate=False))
                    load_next()
                    yield
            V.did(nc.vector.tensor_scalar(UP_T, tot3[:, 0:1], 0.5 / NORM_GAIN, None, ALU.mult))
            m = V.did(nc.vector.tensor_scalar(tmp[6], tot3[:, 0:1], tot3[:, 1:2], 1.0 / HID_GAIN, ALU.mult, ALU.mult))
            V.wait(m)
            V.did(nc.vector.tensor_scalar(FS, tmp[6], tot3[:, 2:3], None, ALU.mult))
            mk["ffnW"] = V.now()

        def tile_scalars(par):
            q = sc[:, par, :]
            return [q[:, i:i + 1] for i in range(5)] + [q[:, 5:5 + CT]]

        def scale_u(par):
            umax, uall, su, comb, half, w_last = tile_scalars(par)
            V.wait(mk["uT"])
            m = V.did(nc.vector.tensor_reduce(umax, uTf[:, :, :], AX.XY, ALU.max, apply_absolute_value=True))
            G.wait(m)
            m = G.did(nc.gpsimd.partition_all_reduce(uall, umax, P, RED.max))
            yield
            V.wait(m)
            m = V.did(nc.vector.tensor_scalar(uall, uall, TINY, None, ALU.max))
            V.wait(m)
            m = V.did(nc.vector.reciprocal(su, uall))
            V.wait(m)
            mk["su"] = V.did(nc.vector.tensor_scalar(su, su, U_TOP, None, ALU.mult))
            yield
            m = V.did(nc.vector.tensor_scalar(comb, uall, IN_INV, 1.0 / U_TOP, ALU.mult, ALU.mult))
            V.wait(m)
            mk["comb", par] = V.did(nc.vector.tensor_scalar(w_last, cw[:, :, HALO], comb, None, ALU.mult))
            yield

        def split_u(par):
            su = tile_scalars(par)[2]
            parts = []
            for k in range(0, KD, 2):
                hi, lo = (uTs[:, i, k:k + 2, :].rearrange("p k t -> p (k t)") for i in range(2))
                A.wait(mk.get("uTs_read"))
                parts += split(hi, lo, uTf[:, k:k + 2, :].rearrange("p k t -> p (k t)"), su, mk["su"])
            mk["uTs"] = parts

        def scale_z(par):
            umax, uall, su, comb, half, w_last = tile_scalars(par)
            V.wait(mk["comb", par], mk["Win", "z"])
            mk["half"] = V.did(nc.vector.tensor_scalar(half, uall, Z_INV, 0.5 / U_TOP, ALU.mult, ALU.mult))

        def project(bank, cols, tok, n, width, channels_out):
            for k in range(KD):
                for wi, ui in ((0, 0), (0, 1), (1, 0)):
                    w = Win[:, wi, k, cols:cols + width]
                    x = uTs[:, ui, k, tok:tok + n]
                    i = nc.tensor.matmul(bank, w if channels_out else x, x if channels_out else w,
                                         start=(k == 0 and wi == ui), stop=(k == KD - 1 and wi == 1))
            return PE.did(i)

        def mixer_in(par, fresh):
            pre_turn, acc_turn, tnh_turn = cycle(range(2)), cycle(range(4)), cycle(range(2))
            umax, uall, su, comb, half, w_last = tile_scalars(par)
            if fresh:
                G.wait(mk.get("S_read"), mk.get("S_done"), *(mk.get(("halo", ct)) for ct in range(CT)))
                m = mk["halo_clear"] = G.did(nc.gpsimd.memset(halo[:, :, :], 0.0))
                mk["S_done"] = G.did(nc.gpsimd.memset(S[:, :], 0.0))
                G.wait(m, mk["S_done"])

            def project_dt():
                PE.wait(mk["uTs"], mk["Win", "dt"])
                b = next(psM_turn)
                bank = psM[b]
                PE.wait(psM_read[b])
                for c in range(NC):
                    p = project(bank[:, c * H:(c + 1) * H], DI + CD, c * P, P, H, False)
                d = [dts[:, i, :] for i in range(10)]

                def bc(v):
                    return v.unsqueeze(1).broadcast_to([P, NC, H])

                def by_chunk(v):
                    return v.rearrange("p (c h) -> p c h", c=NC)

                raw, low, e, s2, q2, pl, dt, a, dldt, s_ = d

                def step(ins):
                    V.wait(V.did(ins))
                v = nc.vector
                V.wait(p, mk["negA"], mk.get("dt_read"), mk["comb", par])
                step(v.scalar_tensor_tensor(by_chunk(raw), by_chunk(bank[:, 0:NC * H]), comb, bc(dtb[:, :]),
                                            ALU.mult, ALU.add))
                psM_read[b] = [V.now()]
                step(v.tensor_scalar(low, raw, -1.0, None, ALU.mult))
                step(v.tensor_tensor(low, low, raw, ALU.min))
                A.wait(V.now())
                V.wait(A.did(nc.scalar.activation(e, low, ACT.Exp)))
                step(v.tensor_scalar(s_, e, 2.0, None, ALU.add))
                step(v.reciprocal(s_, s_))
                step(v.tensor_tensor(s_, s_, e, ALU.mult))
                step(v.tensor_tensor(q2, s_, s_, ALU.mult))
                yield
                step(v.tensor_scalar(pl, q2, 1.0 / 15, None, ALU.mult))
                for odd in (13, 11, 9, 7, 5, 3):
                    step(v.scalar_tensor_tensor(pl, pl, 1.0 / odd, q2, ALU.add, ALU.mult))
                step(v.scalar_tensor_tensor(pl, pl, 1.0, s_, ALU.add, ALU.mult))
                step(v.tensor_scalar(pl, pl, 2.0, None, ALU.mult))
                step(v.scalar_tensor_tensor(dt, raw, 0.0, pl, ALU.max, ALU.add))
                step(v.tensor_tensor(by_chunk(a), by_chunk(dt), bc(negA[:, :]), ALU.mult))
                step(v.tensor_scalar(low, a, A_GAIN, A_FLOOR, ALU.mult, ALU.max))
                V.wait(mk.get("a16_read"))
                step(v.tensor_copy(a16[:, 0, :], low))
                step(v.tensor_tensor(a16[:, 1, :], low, a16[:, 0, :], ALU.subtract))
                mk["a16"] = V.now()

            def decays():
                a, dldt, dt = dts[:, 7, :], dts[:, 8, :], dts[:, 6, :]
                PE.wait(mk["a16"], mk["const"])
                b = next(psM_turn)
                bank = psM[b]
                PE.wait(psM_read[b])
                for i, w in enumerate((tri_le, tri_gt, ones)):
                    p = PE.did(nc.tensor.matmul(bank[:, i * NC * H:(i + 1) * NC * H], w[:, :], a,
                                                start=True, stop=True))
                A.wait(p, mk.get("dec_read"))
                m = A.did(nc.scalar.activation(dec[:, :, :].rearrange("p s n -> p (s n)"), bank[:, 0:3 * NC * H],
                                               ACT.Exp))
                psM_read[b] = [m]
                V.wait(m)
                mk["dec"] = [m, V.did(nc.vector.tensor_tensor(dldt, dec[:, 1, :], dt, ALU.mult))]

            dt_steps = project_dt()
            order = [XT, XT + 1] + list(range(XT))
            live = {}
            LAST = len(order) + 3
            for n in range(LAST):
                if n < len(order):
                    ct = order[n]
                    PE.wait(mk["uTs"], mk["Win", ct])
                    b = next(psM_turn)
                    bank = psM[b]
                    PE.wait(psM_read[b])
                    p = project(bank[:, :], DI + ct * P, 0, T, P, True)
                    s = next(pre_turn)
                    A.wait(pre_read[s])
                    A.wait(p, mk["comb", par])
                    m1 = A.did(nc.scalar.activation(pre[:, s, 1 + HALO:1 + HALO + T], bank[:, :], ACT.Copy, scale=comb))
                    r = next(acc_turn)
                    A.wait(acc_read[r])
                    A.wait(mk["cb"])
                    m2 = A.did(nc.scalar.activation(acc[:, r, :], bank[:, :], ACT.Identity,
                                                    scale=w_last[:, ct:ct + 1], bias=cb[:, ct:ct + 1]))
                    psM_read[b] = [m1, m2]
                    live[n] = dict(s=s, r=r, m=[m1, m2])
                if 0 <= n - 1 < len(order):
                    ct, w = order[n - 1], live[n - 1]
                    V.wait(pre_read[w["s"]], mk.get(("halo", ct)), mk.get("halo_clear"))
                    m = V.did(nc.vector.tensor_copy(pre[:, w["s"], 1:1 + HALO], halo[:, ct, :]))
                    V.wait(m, w["m"])
                    mk["halo", ct] = V.did(nc.vector.tensor_copy(halo[:, ct, :], pre[:, w["s"], 1 + T:1 + T + HALO]))
                    for tap in range(HALO - 1, -1, -1):
                        m = V.did(nc.vector.scalar_tensor_tensor(acc[:, w["r"], :], pre[:, w["s"], 1 + tap:1 + tap + T],
                                                                 cw[:, ct, tap:tap + 1], acc[:, w["r"], :],
                                                                 ALU.mult, ALU.add))
                        V.wait(m)
                    pre_read[w["s"]] = [m, mk["halo", ct]]
                    w["t"] = next(tnh_turn)
                    A.wait(tnh_read[w["t"]])
                    A.wait(m)
                    w["tanh"] = A.did(nc.scalar.activation(tnh[:, w["t"], :], acc[:, w["r"], :], ACT.Tanh))
                if 0 <= n - 2 < len(order):
                    ct, w = order[n - 2], live[n - 2]
                    if ct == XT:
                        dst = BT[:, :]
                        V.wait(mk.get("BT_read"))
                    elif ct == XT + 1:
                        dst = CTt[:, :]
                        V.wait(mk.get("CT_read"))
                    else:
                        dst = acc[:, w["r"], :]
                    V.wait(w["tanh"])
                    m = V.did(nc.vector.scalar_tensor_tensor(dst, tnh[:, w["t"], :], 1.0, acc[:, w["r"], :],
                                                             ALU.add, ALU.mult))
                    tnh_read[w["t"]] = [m]
                    acc_read[w["r"]] = [m]
                    w["silu"] = mk["mixed"] = m
                    if ct >= XT:
                        mk["BT" if ct == XT else "CT"] = m
                if 0 <= n - 3 < len(order):
                    ct, w = order[n - 3], live[n - 3]
                    if ct != XT + 1:
                        PE.wait(w["silu"], mk["const"])
                        src = BT[:, :] if ct == XT else acc[:, w["r"], :]
                        b = next(psM_turn)
                        bank = psM[b]
                        PE.wait(psM_read[b])
                        for c in range(NC):
                            i = nc.tensor.transpose(bank[:, c * P:(c + 1) * P], src[:, c * P:(c + 1) * P], ident[:, :])
                        p = PE.did(i)
                        if ct != XT:
                            acc_read[w["r"]] = mk["acc_turned"] = p
                        dst = Btok[:, :, :] if ct == XT else xtok[:, :, ct * P:(ct + 1) * P]
                        A.wait(p, mk.get("Btok_read") if ct == XT else mk.get("xtok_read"))
                        m = A.did(nc.scalar.activation(dst, bank[:, :].rearrange("p (c n) -> p c n", c=NC), ACT.Copy))
                        psM_read[b] = [m]
                        mk["Btok" if ct == XT else "xtok"] = m
                if n in (6, 7):
                    next(dt_steps, None)
                if n == 9:
                    decays()
                yield

        def hand_over(*marks):
            for ln in (V, A, G):
                ln.wait(*marks)

        def heads(v, n):
            return v.rearrange("p (h d) -> p h d", h=n)

        HG = DI // P
        HW = T // HD
        halves = [slice(w * T, (w + 1) * T) for w in range(DI // T)]

        def cb_product(c):
            tok = slice(c * P, (c + 1) * P)
            b = next(psM_turn)
            PE.wait(psM_read[b], mk["BT"], mk["CT"])
            p = PE.did(nc.tensor.matmul(psM[b][:, 0:P], BT[:, tok], CTt[:, tok], start=True, stop=True))
            mk["BT_read"] = p
            V.wait(p, mk["const"])
            mk["CBm"] = V.did(nc.vector.tensor_tensor(CBm[:, :], psM[b][:, 0:P], tri_le[:, :], ALU.mult))
            psM_read[b] = mk["CBm"]

        def mask_a(c, g):
            s = next(am_turn)
            G.wait(am_read[s], mk["a16"])
            for part in range(2):
                av = a16[:, part, c * H + g * HG:c * H + (g + 1) * HG]
                m = G.did(nc.gpsimd.tensor_tensor(am[:, 2 * s + part, :].rearrange("p (h i) -> p h i", h=HG),
                                                  av.unsqueeze(2).broadcast_to([P, HG, P]),
                                                  tri_le16[:, :].unsqueeze(1).broadcast_to([P, HG, P]), ALU.mult))
            mk["am", g] = (s, m)
            mk["a16_read"] = m

        def scale_x(c):
            ch = slice(c * H, (c + 1) * H)
            V.wait(mk["xtok"], mk["dec"], mk.get("xdt_read"))
            mk["xdt"] = V.did(nc.vector.tensor_tensor(heads(xdt, H), heads(xtok[:, c, :], H),
                                                      dts[:, 6, ch].unsqueeze(2).broadcast_to([P, H, HD]), ALU.mult))
            mk["xtok_read"] = mk["dt_read"] = [mk["xdt"], mk["yd"]]

        def scale_x_state(c):
            ch = slice(c * H, (c + 1) * H)
            G.wait(mk["xtok"], mk["dec"], mk.get("xs_read"), mk.get("yd_read"))
            mk["xs"] = G.did(nc.gpsimd.tensor_tensor(heads(xs, H), heads(xtok[:, c, :], H),
                                                     dts[:, 8, ch].unsqueeze(2).broadcast_to([P, H, HD]), ALU.mult))
            mk["yd"] = G.did(nc.gpsimd.tensor_tensor(heads(yd, H), heads(xtok[:, c, :], H),
                                                     dskip[:, :].unsqueeze(2).broadcast_to([P, H, HD]), ALU.mult))

        def gate(c, par, w):
            half = sc[:, par, 4:5]
            zw = zs2[:, c % 2, halves[w]]
            b = next(psM_turn)
            PE.wait(psM_read[b], mk["uTs"], mk["Win", "z"])
            p = project(psM[b][:, :], w * T, c * P, P, T, False)
            mk["uTs_read"] = p
            A.wait(p, mk["half"], mk.get(("zs_read", c % 2)))
            m = A.did(nc.scalar.activation(zw, psM[b][:, :], ACT.Tanh, scale=half))
            V.wait(m)
            mk["zs", w] = V.did(nc.vector.scalar_tensor_tensor(zw, zw, 1.0, psM[b][:, :], ALU.add, ALU.mult))
            psM_read[b] = mk["zs", w]

        def decay(c):
            for r in range(H // HQ):
                s, m = mk["am", r * HQ // HG]
                b = next(psF_turn)
                PE.wait(psF_read[b], m, mk["const"])
                lo = (r * HQ % HG) * P
                for part in range(2):
                    ins = nc.tensor.matmul(psF[b][:, :], tri_gt16[:, :], am[:, 2 * s + part, lo:lo + T],
                                           start=part == 0, stop=part == 1)
                p = PE.did(ins)
                am_read[s] = p
                Lq = Lm[:, r * HQ:(r + 1) * HQ, :]
                A.wait(p, mk.get("L_read"))
                e = A.did(nc.scalar.activation(Lq, psF[b][:, :].rearrange("p (h i) -> p h i", h=HQ), ACT.Exp,
                                               scale=1.0 / A_GAIN))
                psF_read[b] = e
                V.wait(e, mk["CBm"])
                mk["L", r] = V.did(nc.vector.tensor_tensor(Lq, Lq, CBm[:, :].unsqueeze(1).broadcast_to([P, HQ, P]),
                                                           ALU.mult))

        def y_state(c):
            for w, cols in enumerate(halves):
                b = next(psM_turn)
                PE.wait(psM_read[b], mk["S_done"], mk["CT"])
                p = PE.did(nc.tensor.matmul(psM[b][:, :], CTt[:, c * P:(c + 1) * P], S[:, cols],
                                            start=True, stop=True))
                mk["S_read"] = mk["CT_read"] = p
                grow = dec[:, 0, c * H + w * HW:c * H + (w + 1) * HW]
                V.wait(p, mk.get("y_read"))
                m = V.did(nc.vector.tensor_tensor(heads(y[:, cols], HW), heads(psM[b][:, :], HW),
                                                  grow.unsqueeze(2).broadcast_to([P, HW, HD]), ALU.mult))
                psM_read[b] = m
                mk["y_off", w] = mk["dec_read"] = m

        def new_state(c):
            G.wait(mk["S_read"], mk["S_done"], mk["dec"])
            sd = G.did(nc.gpsimd.tensor_tensor(heads(S[:, :], H), heads(S[:, :], H),
                                               dec[:, 2, c * H:(c + 1) * H].unsqueeze(2).broadcast_to([P, H, HD]),
                                               ALU.mult))
            for cols in halves:
                b = next(psM_turn)
                PE.wait(psM_read[b], mk["xs"], mk["Btok"])
                p = PE.did(nc.tensor.matmul(psM[b][:, :], Btok[:, c, :], xs[:, cols], start=True, stop=True))
                mk["xs_read"] = mk["Btok_read"] = p
                V.wait(p, sd)
                mk["S_done"] = V.did(nc.vector.tensor_tensor(S[:, cols], S[:, cols], psM[b][:, :], ALU.add))
                psM_read[b] = mk["S_done"]
            mk["dec_read"] = [mk["dec_read"], sd]

        def add_skip():
            for w, cols in enumerate(halves):
                G.wait(mk["y_off", w], mk["yd"])
                mk["y_sum", w] = mk["yd_read"] = G.did(nc.gpsimd.tensor_tensor(y[:, cols], y[:, cols], yd[:, cols],
                                                                               ALU.add))

        def y_chunk(c, par, w):
            half, cols = sc[:, par, 4:5], halves[w]
            b = next(psM_turn)
            PE.wait(psM_read[b], mk["xdt"])
            for h in range(w * HW, (w + 1) * HW):
                PE.wait(mk["L", h // HQ])
                ins = nc.tensor.matmul(psM[b][:, (h - w * HW) * HD:(h - w * HW + 1) * HD], Lm[:, h, :],
                                       xdt[:, h * HD:(h + 1) * HD], start=True, stop=True)
            p = PE.did(ins)
            mk["L_read"] = mk["xdt_read"] = p
            V.wait(p, mk["y_sum", w])
            m = V.did(nc.vector.tensor_tensor(y[:, cols], y[:, cols], psM[b][:, :], ALU.add))
            psM_read[b] = m
            V.wait(m, mk["zs", w], mk["half"])
            mk["y"] = V.did(nc.vector.scalar_tensor_tensor(y[:, cols], y[:, cols], half, zs2[:, c % 2, cols],
                                                           ALU.mult, ALU.mult))
            mk["zs_read", c % 2] = mk["y"]

        def rms(c, par):
            ss, r = st[:, par, c, 0:1], st[:, par, c, 1:2]
            A.wait(mk["y"], mk.get("yT_read"))
            squares = yT[:, 0:XT, :].rearrange("p x n -> p (x n)")
            m = A.did(nc.scalar.activation(squares, y, ACT.Square, accum_out=ss))
            G.wait(m)
            m = G.did(nc.gpsimd.tensor_scalar(r, ss, 1.0 / DI, RMS_EPS, ALU.mult, ALU.add))
            G.wait(m)
            m = G.did(nc.gpsimd.tensor_tensor(r, r, minus_half[:, :], ALU.pow))
            A.wait(m)
            mk["yn"] = A.did(nc.scalar.activation(y, y, ACT.Copy, scale=r))

        def row_stats(c, par, col, h):
            s6, mv, r, nm = (st[:, par, c, a:b] for a, b in ((col, col + 6), (14, 16), (12, 13), (13, 14)))
            V.wait(h)
            m = V.did(nc.vector.bn_stats(s6, x1[:, c, :]))
            V.wait(m)
            m = V.did(nc.vector.bn_aggr(mv, s6))
            G.wait(m)
            m = G.did(nc.gpsimd.tensor_scalar(r, mv[:, 1:2], LN_EPS, None, ALU.add))
            G.wait(m)
            m = G.did(nc.gpsimd.tensor_tensor(r, r, minus_half[:, :], ALU.pow))
            G.wait(m)
            return G.did(nc.gpsimd.tensor_scalar(nm, mv[:, 0:1], r, -1.0, ALU.mult, ALU.mult))

        def normalise(c, par, stats):
            r, nm = st[:, par, c, 12:13], st[:, par, c, 13:14]
            A.wait(stats)
            return A.did(nc.scalar.activation(x1[:, c, :], x1[:, c, :], ACT.Identity, bias=nm, scale=r))

        def take_bank(c):
            return (next(psF_turn), psF, psF_read) if c == NC - 1 else (next(psM_turn), psM, psM_read)

        def turn_y(c):
            XB = T // P
            for w in range(XT // XB):
                b, ps, read = take_bank(c)
                PE.wait(read[b], mk["yn"])
                for x in range(XB):
                    ins = nc.tensor.transpose(ps[b][:, x * P:(x + 1) * P], y[:, (XB * w + x) * P:(XB * w + x + 1) * P],
                                              ident[:, :])
                p = PE.did(ins)
                mk["y_read"] = p
                hi, lo = (yT[:, i * XT + XB * w:i * XT + XB * w + XB, :].rearrange("p x n -> p (x n)")
                          for i in range(2))
                A.wait(p, mk.get("yT_read"))
                m = A.did(nc.scalar.activation(hi, ps[b][:, :], ACT.Copy, scale=NORM_GAIN))
                V.wait(m)
                mk["yT", w] = V.did(nc.vector.scalar_tensor_tensor(lo, ps[b][:, :], NORM_GAIN, hi,
                                                                   ALU.mult, ALU.subtract))
                read[b] = mk["yT", w]

        def load_res(t, c):
            LR[c % 2].wait(mk.get(("res_read", c % 2)))
            mk["res", c] = LR[c % 2].did(nc.sync.dma_start(res[:, c % 2, :], u_v[:, t, c, :]))

        def project_out(c, par):
            b, ps, read = take_bank(c)
            PE.wait(read[b], mk["Wout"])
            for x in range(XT):
                PE.wait(mk["yT", x // (T // P)])
                for yi, wi in ((0, 0), (0, 1), (1, 0)):
                    ins = nc.tensor.matmul(ps[b][:, :], yT[:, yi * XT + x, :], Wout[:, wi, x, :],
                                           start=(x == 0 and yi == wi), stop=(x == XT - 1 and yi == 1))
            p = PE.did(ins)
            mk["yT_read"] = p
            V.wait(p, mk["res", c], mk.get(("stored", c)))
            h = V.did(nc.vector.scalar_tensor_tensor(x1[:, c, :], ps[b][:, :], OUT_INV, res[:, c % 2, :],
                                                     ALU.mult, ALU.add))
            read[b] = h
            mk["res_read", c % 2] = h
            mk["x1_stats", c] = row_stats(c, par, 2, h)

        def turn_x1(c):
            b, ps, read = take_bank(c)
            PE.wait(read[b], mk["x1", c])
            for k in range(KD):
                ins = nc.tensor.transpose(ps[b][:, k * P:(k + 1) * P], x1[:, c, k * P:(k + 1) * P], ident[:, :])
            p = PE.did(ins)
            hi, lo = (x1T[:, i, :, c * P:(c + 1) * P] for i in range(2))
            bv = ps[b][:, :].rearrange("p (k n) -> p k n", k=KD)
            A.wait(p, mk.get("x1T_read"))
            m = A.did(nc.scalar.activation(hi, bv, ACT.Copy, scale=NORM_GAIN))
            V.wait(m)
            l = V.did(nc.vector.scalar_tensor_tensor(lo, bv, NORM_GAIN, hi, ALU.mult, ALU.subtract))
            read[b] = l
            mk["x1T_new", c] = l

        def ffn_up(half):
            live = {}
            for n in range(EH + 1):
                if n < EH:
                    e = half * EH + n
                    PE.wait(mk["x1T"], mk.get("ffnW"))
                    ps = []
                    for Wm in (Wup, Wgate):
                        b = next(psF_turn)
                        bank = psF[b]
                        PE.wait(psF_read[b])
                        for k in range(KD):
                            for i in range(2):
                                ins = nc.tensor.matmul(bank[:, :], Wm[:, k, e * P:(e + 1) * P], x1T[:, i, k, :],
                                                       start=(k == 0 and i == 0), stop=(k == KD - 1 and i == 1))
                        ps.append((bank, b, PE.did(ins)))
                    mk["x1T_read"] = ps[1][2]
                    (Ub, ub, up), (Gb, gb, gp) = ps
                    t = next(fth_turn)
                    A.wait(fth_read[t])
                    A.wait(up)
                    m = A.did(nc.scalar.activation(fth[:, t, :], Ub[:, :], ACT.Tanh, scale=UP_T))
                    live[n] = (t, m, Ub, ub, Gb, gb, gp)
                if n >= 1:
                    t, m, Ub, ub, Gb, gb, gp = live[n - 1]
                    q = next(fp_turn)
                    V.wait(fp_read[q])
                    V.wait(m)
                    m = V.did(nc.vector.scalar_tensor_tensor(fp[:, q, :], fth[:, t, :], 1.0, Ub[:, :],
                                                             ALU.add, ALU.mult))
                    fth_read[t] = [m]
                    psF_read[ub] = [m]
                    f = next(fh_turn)
                    V.wait(fh_read[f])
                    V.wait(m, gp)
                    m = V.did(nc.vector.scalar_tensor_tensor(fh[:, f, :], fp[:, q, :],
                                                             0.5 * HID_GAIN / NORM_GAIN ** 2, Gb[:, :],
                                                             ALU.mult, ALU.mult))
                    fp_read[q] = [m]
                    psF_read[gb] = [m]
                    A.wait(m, mk.get("hid_read"))
                    h = A.did(nc.scalar.activation(hid[:, 0, n - 1, :], fh[:, f, :], ACT.Copy))
                    V.wait(h, m, mk.get("hid_read"))
                    l = V.did(nc.vector.tensor_tensor(hid[:, 1, n - 1, :], fh[:, f, :], hid[:, 0, n - 1, :],
                                                      ALU.subtract))
                    fh_read[f] = [h, l]
                    mk["hid", n - 1] = [h, l]
                yield

        def ffn_down(half, c):
            b = next(psF_turn)
            bank = psF[b]
            PE.wait(psF_read[b])
            for n in range(EH):
                PE.wait(mk["hid", n])
                for i in range(2):
                    ins = nc.tensor.matmul(bank[:, :], hid[:, i, n, c * P:(c + 1) * P], Wdown[:, half * EH + n, :],
                                           start=(n == 0 and i == 0), stop=(n == EH - 1 and i == 1))
            p = PE.did(ins)
            mk["hid_read"] = p
            V.wait(p, mk["x1", c])
            m = V.did(nc.vector.scalar_tensor_tensor(x1[:, c, :], bank[:, :], FS, x1[:, c, :], ALU.mult, ALU.add))
            psF_read[b] = [m]
            mk["x1", c] = m

        def ffn_last(c, par):
            ffn_down(1, c)
            mk["out_stats", c] = row_stats(c, 1 - par, 2, mk["x1", c])

        def ffn_store(c, par, t):
            n = normalise(c, 1 - par, mk["out_stats", c])
            ST[c].wait(n)
            mk["stored", c] = ST[c].did(nc.sync.dma_start(out_v[:, t, c, :], x1[:, c, :]))

        def ffn_first():
            mk["x1T"] = [mk.get(("x1T_new", c)) for c in range(NC)]
            yield from ffn_up(0)
            for c in range(NC):
                ffn_down(0, c)
                yield
            yield from ffn_up(1)

        def run(gen):
            for _ in gen:
                pass

        def phase2_masks():
            G.wait(mk["acc_turned"], mk["mixed"])
            mask_a(0, 0)
            mask_a(0, 1)
            scale_x_state(0)

        def phase2(par, mixer_t, ffn_t, ffn_rest, early, filler=None):
            next_u = scale_u(1 - par)
            ahead = 1 if early else 0
            load_res(mixer_t, 0)
            load_res(mixer_t, 1)
            scale_z(par)

            def spare():
                if filler:
                    next(filler, None)

            cb_product(0)
            next(ffn_rest, None)
            next(ffn_rest, None)
            gate(0, par, 0)
            run(ffn_rest)
            gate(0, par, 1)
            hand_over(mk["acc_turned"], V.now(), A.now())
            scale_x(0)
            decay(0)
            for c in range(NC):
                last = c + 1 == NC
                f = c + ahead
                y_state(c)
                new_state(c)
                add_skip()
                spare()
                if not last:
                    mask_a(c + 1, 0)
                if c == 0 and ffn_t is not None and ahead:
                    ffn_last(0, par)
                    ffn_store(0, par, ffn_t)
                if c:
                    mk["x1", c - 1] = normalise(c - 1, par, mk["x1_stats", c - 1])
                if early:
                    next(next_u, None)
                if last and early:
                    hand_over(PE.now(), G.now())
                    next(early)
                y_chunk(c, par, 0)
                if c:
                    turn_x1(c - 1)
                y_chunk(c, par, 1)
                rms(c, par)
                spare()
                if c >= NC - 2:
                    spare()
                if last:
                    if early:
                        next(early)
                        next(early)
                else:
                    cb_product(c + 1)
                    gate(c + 1, par, 0)
                    mask_a(c + 1, 1)
                if ffn_t is not None and f < NC:
                    ffn_last(f, par)
                turn_y(c)
                spare()
                if ffn_t is not None and f < NC:
                    ffn_store(f, par, ffn_t)
                if not last:
                    gate(c + 1, par, 1)
                    scale_x(c + 1)
                    scale_x_state(c + 1)
                    decay(c + 1)
                elif early:
                    next(early)
                spare()
                if early and c == NC - 2:
                    split_u(1 - par)
                project_out(c, par)
                spare()
                if c + 2 < NC:
                    load_res(mixer_t, c + 2)
            if early:
                next(early)
            mk["x1", NC - 1] = normalise(NC - 1, par, mk["x1_stats", NC - 1])
            if early:
                next(early)
            turn_x1(NC - 1)

        def tile(par, mixer_t, ffn_t, inputs, early):
            if early:
                load_uT(mixer_t + 1, mk["uTs"])
            ffn = ffn_first()
            hand_over(mk["L_read"])
            next(inputs)
            drain((inputs, MIXER_STEPS - EARLY - 1), (ffn, FFN_STEPS - 4))
            phase2_masks()
            phase2(par, mixer_t, ffn_t, ffn, early)

        MIXER_STEPS = CT + 3
        EARLY = 6
        FFN_STEPS = 2 * (EH + 1) + NC
        setup()
        from_in, ffn_weight_steps = in_weights(), ffn_weights()
        for _ in range(3):
            next(from_in)
        even = mixer_in(0, True)
        drain((even, XT + 1), (from_in, XT + 5))
        drain((even, MIXER_STEPS - XT - 1), (from_in, 5))
        phase2_masks()
        drain((chain(from_in, out_weights()), 8), (ffn_weight_steps, 6))
        odd = mixer_in(1, False)
        phase2(0, 0, None, iter(()), odd, ffn_weight_steps)
        run(ffn_weight_steps)
        barrier()
        with nc.Fori(0, NT // 2 - 1) as i:
            even, next_odd = mixer_in(0, True), mixer_in(1, False)
            tile(1, 2 * i + 1, 2 * i, odd, even)
            tile(0, 2 * i + 2, 2 * i + 1, even, next_odd)
            barrier()
        tile(1, NT - 1, NT - 2, next_odd, None)
        run(ffn_first())
        for c in range(NC):
            ffn_last(c, 0)
            ffn_store(c, 0, NT - 1)
        for c in range(NC):
            SP.wait(ST[c].now())

_INS = ["u", "uT", "W_inT", "conv_w", "conv_b", "dt_bias", "A_log", "Dp", "norm_w", "W_outT", "W_upT", "W_gateT",
        "W_downT"]


def kernel(**inputs):
    import numpy as np
    import concourse.bacc as bacc
    from concourse import mybir as _mybir
    from concourse.bass_utils import run_bass_kernel_spmd

    g = {k: np.asarray(v) for k, v in inputs.items()}
    u = g["L0_attn_u"]
    rows = {
        "u": u,
        "uT": u.reshape(-1, u.shape[-1]).T,
        "W_inT": g["L0_attn_W_in"].T,
        "conv_w": g["L0_attn_conv_w"],
        "conv_b": g["L0_attn_conv_b"],
        "dt_bias": g["L0_attn_dt_bias"],
        "A_log": g["L0_attn_A_log"],
        "Dp": g["L0_attn_Dp"],
        "norm_w": g["L0_attn_norm_w"],
        "W_outT": g["L0_attn_W_out"].T,
        "W_upT": g["L0_ffn_W_up"].T,
        "W_gateT": g["L0_ffn_W_gate"].T,
        "W_downT": g["L0_ffn_W_down"].T,
    }
    nc = bacc.Bacc("TRN2", target_bir_lowering=False, num_devices=1)
    arrays, args = {}, []
    for name in _INS:
        a = np.ascontiguousarray(rows[name])
        arrays[f"in_{name}"] = a
        args.append(nc.dram_tensor(f"in_{name}", a.shape, _mybir.dt.from_np(a.dtype), kind="ExternalInput").ap())
    args.append(nc.dram_tensor("out_y", u.shape, _mybir.dt.from_np(u.dtype), kind="ExternalOutput").ap())
    build(nc, *args)
    r = run_bass_kernel_spmd(nc, [arrays], core_ids=[0])
    return r.results[0]["out_y"]
```
